# Optimizing a Trainium2 kernel written in Bass

```python
import numpy as np
import jax
import jax.numpy as jnp

def _softmax(x, axis=-1):
    return jax.nn.softmax(x, axis=axis)

def _gelu(x):
    return jax.nn.gelu(x, approximate=True)

def _silu(x):
    return jax.nn.silu(x)

def _sigmoid(x):
    return jax.nn.sigmoid(x)

def _layernorm(x, axis=-1, eps=1e-05):
    m = jnp.mean(x, axis=axis, keepdims=True)
    v = jnp.var(x, axis=axis, keepdims=True)
    return (x - m) / jnp.sqrt(v + eps)

def _scatter_add(tgt, idx, src, axis=0):
    return tgt.at[idx].add(src)

def _segment_sum(src, seg, n):
    return jax.ops.segment_sum(src, seg, n)
kernel_name = 'mk_seq_preln_d2_jaxref_r8_4a1d2a'

def setup_inputs(seed: int=0):
    np.random.seed(seed)
    _w = jnp.asarray

    def _L0_attn_setup():
        import math
        import jax, jax.numpy as jnp
        import numpy as np
        NUM_HEADS = 16
        NUM_BUCKETS = 32

        def _relative_position_bucket(relative_position):
            num_buckets = NUM_BUCKETS
            n = jnp.maximum(-relative_position, 0)
            max_exact = num_buckets // 2
            is_small = n < max_exact
            n_safe = jnp.maximum(n, 1).astype(jnp.float32)
            val_if_large = max_exact + (jnp.log(n_safe / max_exact) / math.log(num_buckets / max_exact) * (num_buckets - max_exact)).astype(jnp.int32)
            val_if_large = jnp.minimum(val_if_large, num_buckets - 1)
            return jnp.where(is_small, n, val_if_large)
        key = jax.random.key(seed)
        ks = jax.random.split(key, 8)
        B, S, D = (2, 256, 128)
        s = 1.0 / math.sqrt(D)
        return {'hidden_states': jax.random.normal(ks[0], (B, S, D), jnp.float32), 'Wq': jax.random.normal(ks[1], (D, D), jnp.float32) * s, 'bq': jnp.zeros((D,), jnp.float32), 'Wk': jax.random.normal(ks[2], (D, D), jnp.float32) * s, 'bk': jnp.zeros((D,), jnp.float32), 'Wv': jax.random.normal(ks[3], (D, D), jnp.float32) * s, 'bv': jnp.zeros((D,), jnp.float32), 'rel_bias': jax.random.normal(ks[4], (NUM_BUCKETS, NUM_HEADS), jnp.float32) * 0.02}
    _L0_attn_in = _L0_attn_setup()

    def _L0_ffn_setup():
        import jax, jax.numpy as jnp
        import numpy as np
        DIM = 128

        def _reference_tuple_inner(x, W_r, W_k, W_v, mu_r, mu_k):
            B, T, C = x.shape
            x_prev = jnp.concatenate([jnp.zeros((B, 1, C), x.dtype), x[:, :-1, :]], axis=1)
            xr = mu_r * x + (1.0 - mu_r) * x_prev
            xk = mu_k * x + (1.0 - mu_k) * x_prev
            r = jax.nn.sigmoid(jnp.einsum('btc,dc->btd', xr, W_r))
            k = jnp.einsum('btc,dc->btd', xk, W_k)
            k_act = jnp.square(jax.nn.relu(k))
            out = r * jnp.einsum('btc,dc->btd', k_act, W_v)
            new_state = x[:, -1, :]
            return (out, new_state)
        key = jax.random.key(seed)
        ks = jax.random.split(key, 6)
        B, T, C = (8, 256, DIM)
        x = jax.random.normal(ks[0], (B, T, C), dtype=jnp.float32)
        s = 1.0 / np.sqrt(C)
        W_r = jax.random.uniform(ks[1], (C, C), jnp.float32, -s, s)
        W_k = jax.random.uniform(ks[2], (C, C), jnp.float32, -s, s)
        W_v = jax.random.uniform(ks[3], (C, C), jnp.float32, -s, s)
        mu_r = jax.random.uniform(ks[4], (C,), jnp.float32)
        mu_k = jax.random.uniform(ks[5], (C,), jnp.float32)
        return {'x': x, 'W_r': W_r, 'W_k': W_k, 'W_v': W_v, 'mu_r': mu_r, 'mu_k': mu_k}
    _L0_ffn_in = _L0_ffn_setup()

    def _L1_attn_setup():
        import jax, jax.numpy as jnp
        import numpy as np
        L, B, D, FF = (512, 4, 128, 512)
        EPS = 1e-05

        def layer_norm(x, w, b):
            mu = jnp.mean(x, axis=-1, keepdims=True)
            var = jnp.var(x, axis=-1, keepdims=True)
            return (x - mu) * jax.lax.rsqrt(var + EPS) * w + b

        def spiral_conv(h, lmlg, theta, last_conv_init):
            seq_len = h.shape[0]
            gamma = jnp.exp(-jnp.exp(lmlg))
            c = gamma * jnp.exp(1j * theta.astype(jnp.complex64))
            n = jnp.arange(seq_len)[:, None]
            filt = jnp.power(c[None, :], n)
            filt_fft = jnp.fft.fft(filt, n=2 * seq_len, axis=0)
            x_fft = jnp.fft.fft(h.astype(jnp.complex64), n=2 * seq_len, axis=0)
            conv = jnp.fft.ifft(filt_fft[:, None, :] * x_fft, axis=0)[:seq_len]
            last_conv = jax.lax.stop_gradient(jnp.broadcast_to(last_conv_init[None, :], (h.shape[1], h.shape[2]))).astype(jnp.complex64)
            conv_with_past = conv + last_conv[None, :, :] * filt[:, None, :] * c[None, None, :]
            return conv_with_past.real * h
        key = jax.random.key(seed)
        ks = jax.random.split(key, 10)
        return {'x': jax.random.normal(ks[0], (L, B, D), dtype=jnp.float32), 'lmlg': jax.random.normal(ks[1], (D,), dtype=jnp.float32), 'theta': jax.random.normal(ks[2], (D,), dtype=jnp.float32), 'last_conv_init': jax.random.normal(ks[3], (D,), dtype=jnp.float32), 'ln_w': jax.random.normal(ks[4], (D,), dtype=jnp.float32) * 0.1 + 1.0, 'ln_b': jax.random.normal(ks[5], (D,), dtype=jnp.float32) * 0.1, 'w1': jax.random.normal(ks[6], (D, FF), dtype=jnp.float32) / np.sqrt(D), 'b1': jax.random.normal(ks[7], (FF,), dtype=jnp.float32) * 0.02, 'w2': jax.random.normal(ks[8], (FF, D), dtype=jnp.float32) / np.sqrt(FF), 'b2': jax.random.normal(ks[9], (D,), dtype=jnp.float32) * 0.02}
    _L1_attn_in = _L1_attn_setup()

    def _L1_ffn_setup():
        import jax, jax.numpy as jnp
        import numpy as np
        DIM = 128
        HIDDEN = 352
        NUM_EXPERTS = 8
        TOP_K = 2
        BATCH, SEQ = (4, 256)
        key = jax.random.key(seed)
        ks = jax.random.split(key, 5)
        x = jax.random.normal(ks[0], (BATCH, SEQ, DIM), dtype=jnp.float32)
        gate_w = jax.random.normal(ks[1], (NUM_EXPERTS, DIM), dtype=jnp.float32) * 0.02
        w1 = jax.random.normal(ks[2], (NUM_EXPERTS, HIDDEN, DIM), dtype=jnp.float32) * 0.02
        w3 = jax.random.normal(ks[3], (NUM_EXPERTS, HIDDEN, DIM), dtype=jnp.float32) * 0.02
        w2 = jax.random.normal(ks[4], (NUM_EXPERTS, DIM, HIDDEN), dtype=jnp.float32) * 0.02
        return {'x': x, 'gate_w': gate_w, 'w1': w1, 'w3': w3, 'w2': w2}
    _L1_ffn_in = _L1_ffn_setup()
    _d = {'L0_attn_hidden_states': _L0_attn_in['hidden_states'], 'L0_attn_Wq': _L0_attn_in['Wq'], 'L0_attn_bq': _L0_attn_in['bq'], 'L0_attn_Wk': _L0_attn_in['Wk'], 'L0_attn_bk': _L0_attn_in['bk'], 'L0_attn_Wv': _L0_attn_in['Wv'], 'L0_attn_bv': _L0_attn_in['bv'], 'L0_attn_rel_bias': _L0_attn_in['rel_bias'], 'L0_ffn_W_r': _L0_ffn_in['W_r'], 'L0_ffn_W_k': _L0_ffn_in['W_k'], 'L0_ffn_W_v': _L0_ffn_in['W_v'], 'L0_ffn_mu_r': _L0_ffn_in['mu_r'], 'L0_ffn_mu_k': _L0_ffn_in['mu_k'], 'L1_attn_lmlg': _L1_attn_in['lmlg'], 'L1_attn_theta': _L1_attn_in['theta'], 'L1_attn_last_conv_init': _L1_attn_in['last_conv_init'], 'L1_attn_ln_w': _L1_attn_in['ln_w'], 'L1_attn_ln_b': _L1_attn_in['ln_b'], 'L1_attn_w1': _L1_attn_in['w1'], 'L1_attn_b1': _L1_attn_in['b1'], 'L1_attn_w2': _L1_attn_in['w2'], 'L1_attn_b2': _L1_attn_in['b2'], 'L1_ffn_gate_w': _L1_ffn_in['gate_w'], 'L1_ffn_w1': _L1_ffn_in['w1'], 'L1_ffn_w3': _L1_ffn_in['w3'], 'L1_ffn_w2': _L1_ffn_in['w2']}
    _x0 = _d['L0_attn_hidden_states']
    _d['L0_attn_hidden_states'] = jax.random.normal(jax.random.fold_in(jax.random.key(seed), 1), (2, 1024, 128), dtype=_x0.dtype)
    del _x0
    return _d

def reference(L0_attn_hidden_states, L0_attn_Wq, L0_attn_bq, L0_attn_Wk, L0_attn_bk, L0_attn_Wv, L0_attn_bv, L0_attn_rel_bias, L0_ffn_W_r, L0_ffn_W_k, L0_ffn_W_v, L0_ffn_mu_r, L0_ffn_mu_k, L1_attn_lmlg, L1_attn_theta, L1_attn_last_conv_init, L1_attn_ln_w, L1_attn_ln_b, L1_attn_w1, L1_attn_b1, L1_attn_w2, L1_attn_b2, L1_ffn_gate_w, L1_ffn_w1, L1_ffn_w3, L1_ffn_w2):

    def _L0_attn_ref(hidden_states, Wq, bq, Wk, bk, Wv, bv, rel_bias):
        import math
        import jax, jax.numpy as jnp
        import numpy as np
        NUM_HEADS = 16
        NUM_BUCKETS = 32

        def _relative_position_bucket(relative_position):
            num_buckets = NUM_BUCKETS
            n = jnp.maximum(-relative_position, 0)
            max_exact = num_buckets // 2
            is_small = n < max_exact
            n_safe = jnp.maximum(n, 1).astype(jnp.float32)
            val_if_large = max_exact + (jnp.log(n_safe / max_exact) / math.log(num_buckets / max_exact) * (num_buckets - max_exact)).astype(jnp.int32)
            val_if_large = jnp.minimum(val_if_large, num_buckets - 1)
            return jnp.where(is_small, n, val_if_large)
        B, S, D = hidden_states.shape
        H = NUM_HEADS
        dh = D // H
        q = (hidden_states @ Wq + bq).reshape(B, S, H, dh)
        k = (hidden_states @ Wk + bk).reshape(B, S, H, dh)
        v = (hidden_states @ Wv + bv).reshape(B, S, H, dh)
        scores = jnp.einsum('bqhd,bkhd->bhqk', q, k) / math.sqrt(dh)
        ctx_pos = jnp.arange(S)[:, None]
        mem_pos = jnp.arange(S)[None, :]
        buckets = _relative_position_bucket(mem_pos - ctx_pos)
        bias = rel_bias[buckets]
        bias = jnp.transpose(bias, (2, 0, 1))
        scores = scores + bias[None]
        attn = jax.nn.softmax(scores, axis=-1)
        context = jnp.einsum('bhqk,bkhd->bqhd', attn, v).reshape(B, S, D)
        return context

    def _L0_ffn_ref(x, W_r, W_k, W_v, mu_r, mu_k):
        import jax, jax.numpy as jnp
        import numpy as np
        DIM = 128

        def _reference_tuple_inner(x, W_r, W_k, W_v, mu_r, mu_k):
            B, T, C = x.shape
            x_prev = jnp.concatenate([jnp.zeros((B, 1, C), x.dtype), x[:, :-1, :]], axis=1)
            xr = mu_r * x + (1.0 - mu_r) * x_prev
            xk = mu_k * x + (1.0 - mu_k) * x_prev
            r = jax.nn.sigmoid(jnp.einsum('btc,dc->btd', xr, W_r))
            k = jnp.einsum('btc,dc->btd', xk, W_k)
            k_act = jnp.square(jax.nn.relu(k))
            out = r * jnp.einsum('btc,dc->btd', k_act, W_v)
            new_state = x[:, -1, :]
            return (out, new_state)
        return _reference_tuple_inner(x, W_r, W_k, W_v, mu_r, mu_k)[0]

    def _L1_attn_ref(x, lmlg, theta, last_conv_init, ln_w, ln_b, w1, b1, w2, b2):
        import jax, jax.numpy as jnp
        import numpy as np
        L, B, D, FF = (512, 4, 128, 512)
        EPS = 1e-05

        def layer_norm(x, w, b):
            mu = jnp.mean(x, axis=-1, keepdims=True)
            var = jnp.var(x, axis=-1, keepdims=True)
            return (x - mu) * jax.lax.rsqrt(var + EPS) * w + b

        def spiral_conv(h, lmlg, theta, last_conv_init):
            seq_len = h.shape[0]
            gamma = jnp.exp(-jnp.exp(lmlg))
            c = gamma * jnp.exp(1j * theta.astype(jnp.complex64))
            n = jnp.arange(seq_len)[:, None]
            filt = jnp.power(c[None, :], n)
            filt_fft = jnp.fft.fft(filt, n=2 * seq_len, axis=0)
            x_fft = jnp.fft.fft(h.astype(jnp.complex64), n=2 * seq_len, axis=0)
            conv = jnp.fft.ifft(filt_fft[:, None, :] * x_fft, axis=0)[:seq_len]
            last_conv = jax.lax.stop_gradient(jnp.broadcast_to(last_conv_init[None, :], (h.shape[1], h.shape[2]))).astype(jnp.complex64)
            conv_with_past = conv + last_conv[None, :, :] * filt[:, None, :] * c[None, None, :]
            return conv_with_past.real * h
        h = layer_norm(x, ln_w, ln_b)
        x = spiral_conv(h, lmlg, theta, last_conv_init) + x
        h = layer_norm(x, ln_w, ln_b)
        h = jax.nn.silu(h @ w1 + b1) @ w2 + b2
        return x + h

    def _L1_ffn_ref(x, gate_w, w1, w3, w2):
        import jax, jax.numpy as jnp
        import numpy as np
        DIM = 128
        HIDDEN = 352
        NUM_EXPERTS = 8
        TOP_K = 2
        BATCH, SEQ = (4, 256)
        orig_shape = x.shape
        xf = x.reshape(-1, x.shape[-1])
        T = xf.shape[0]
        E, K = (gate_w.shape[0], TOP_K)
        scores = jax.nn.softmax(xf @ gate_w.T, axis=-1)
        expert_weights, expert_indices = jax.lax.top_k(scores, K)
        expert_weights = expert_weights / jnp.sum(expert_weights, axis=-1, keepdims=True)
        x_rep = jnp.repeat(xf, K, axis=0)
        flat_idx = expert_indices.reshape(-1)
        y = jnp.zeros_like(x_rep)
        for e in range(E):
            m = (flat_idx == e)[:, None]
            xe = jnp.where(m, x_rep, 0.0)
            h = jax.nn.silu(xe @ w1[e].T) * (xe @ w3[e].T)
            out = h @ w2[e].T
            y = y + jnp.where(m, out, 0.0)
        y = jnp.sum(y.reshape(T, K, -1) * expert_weights[..., None], axis=1)
        return y.reshape(orig_shape)
    x = L0_attn_hidden_states
    x = x + _L0_attn_ref(_layernorm(x, axis=-1), L0_attn_Wq, L0_attn_bq, L0_attn_Wk, L0_attn_bk, L0_attn_Wv, L0_attn_bv, L0_attn_rel_bias)
    x = x + _L0_ffn_ref(_layernorm(x, axis=-1), L0_ffn_W_r, L0_ffn_W_k, L0_ffn_W_v, L0_ffn_mu_r, L0_ffn_mu_k)
    x = x + _L1_attn_ref(_layernorm(x, axis=-1), L1_attn_lmlg, L1_attn_theta, L1_attn_last_conv_init, L1_attn_ln_w, L1_attn_ln_b, L1_attn_w1, L1_attn_b1, L1_attn_w2, L1_attn_b2)
    x = x + _L1_ffn_ref(_layernorm(x, axis=-1), L1_ffn_gate_w, L1_ffn_w1, L1_ffn_w3, L1_ffn_w2)
    return x

_drawn_inputs = setup_inputs


def setup_inputs(seed=0):
    import zlib

    import numpy as np

    out = dict(_drawn_inputs(seed))
    spreads = {'L0_attn_bq': (0.0, 0.774), 'L0_attn_bk': (0.0, 0.8), 'L0_attn_bv': (0.0, 0.1)}
    factors = {'L0_attn_rel_bias': 8.0,
     'L0_ffn_W_r': 2.864,
     'L0_ffn_mu_r': 5.726,
     'L1_attn_b1': 8.0,
     'L1_attn_b2': 6.997,
     'L1_ffn_gate_w': 8.0,
     'L1_ffn_w1': 8.0,
     'L1_ffn_w3': 8.0,
     'L1_ffn_w2': 8.0}
    for name, (base, spread) in spreads.items():
        noise = np.random.default_rng([zlib.crc32(name.encode()), seed]).standard_normal(out[name].shape)
        drawn = base * np.exp(spread * noise) if base else spread * noise
        out[name] = jnp.asarray(drawn.astype(out[name].dtype))
    for name, factor in factors.items():
        out[name] = (out[name] * factor).astype(out[name].dtype)
    return out
```

```python
import concourse.bass as bass
from concourse import mybir
from concourse.alu_op_type import AluOpType as ALU
from contextlib import ExitStack
import numpy as np

F32 = mybir.dt.float32
F32R = mybir.dt.float32r
U32 = mybir.dt.uint32
ACT = mybir.ActivationFunctionType
AX = mybir.AxisListType

B, S, D = 2, 1024, 128
H = 16
DH = D // H
NB = 32
NBLK = S // 128
PAIRS = B * H // 2
BAND = 32
EPS = 1e-5

DIAG, EDGE, STEP = 0, 256, 416
WCOLS = 544
ROW_STEP = 32
ROW_MAX = 46


def buckets(n):
    n = np.maximum(n, 0)
    large = 16 + (np.log(np.maximum(n, 1).astype(np.float32) / np.float32(16)) / np.float32(np.log(2.0))
                  * np.float32(16)).astype(np.int32)
    return np.where(n < 16, n, np.minimum(large, NB - 1))


def bias_selectors():
    sel = np.zeros((NB, WCOLS), np.float32)
    for at, distances, base in ((DIAG, range(-127, 128), 0), (EDGE, range(1, 160), NB - 1), (STEP, [BAND] * 128, 0)):
        for c, n in enumerate(distances):
            sel[buckets(np.array(n)), at + c] += 1
            sel[base, at + c] -= 1
    return sel


def step_rows():
    rows = np.zeros((16, S), np.float32)
    for r in range(1, NBLK):
        rows[2 * (r - 1):2 * r, :128 * r] = 1
    rows[14:16] = 1
    return rows


class Pair:

    def __init__(self, turn, r):
        self.turn, self.r = turn, r
        self.set = r % 3
        self.use = r // 3 + turn

    def __add__(self, n):
        return Pair(self.turn, self.r + n)

    @property
    def n(self):
        return self.turn * 3 + self.r


class Chain:

    def __init__(self, eng, sem, base=0):
        self.eng, self.sem, self.base, self.k = eng, sem, base, 0

    def mark(self, ins):
        self.k += 1
        return ins.then_inc(self.sem, 1)

    def settle(self):
        self.eng.wait_ge(self.sem, self.base + self.k)


def attention_block(nc, ctx, io, X, CTXH, ID, later_loads, loaded):
    (x, Wq, bq, Wk, bk, Wv, bv, rel, ident_d, flip_d, sel_d, rows_d) = io

    def dram(name, shape):
        return nc.dram_tensor(name, shape, F32, kind="Internal").ap()

    QD, KD = dram("q_parts", (2, B * D, S)), dram("k_parts", (2, B * D, S))
    LD = dram("step_values", (2 * H, 16, S))
    WD = dram("bias_vectors", (2 * H, 3, WCOLS))
    MD = dram("row_maxima", (PAIRS, 2, 2, S))

    def sb(name, shape, dt=F32):
        return ctx.enter_context(nc.sbuf_tensor("sb_" + name, shape, dt))

    def pb(name, shape):
        return ctx.enter_context(nc.psum_tensor(name, shape, F32))

    def sem(name):
        return ctx.enter_context(nc.semaphore(name))

    XT = sb("xn_T", [128, B * S])
    XN = sb("xn", [128, 2, 4, D])
    WQ, WK, WV = sb("wq", [D, D]), sb("wk", [D, D]), sb("wv", [D, D])
    BQ, BK, BV = sb("bq_col", [D, 1]), sb("bk_col", [D, 1]), sb("bv_rows", [128, D])
    REL, SEL = sb("rel", [NB, 2 * H]), sb("sel", [NB, WCOLS])
    FLIP, FLIPR = sb("flip", [128, 128]), sb("flip_r", [128, 128], F32R)
    ROWS = sb("rows", [48, S])
    W3 = sb("bias_w", [2 * H, 3, WCOLS])
    ZERO = sb("zeros", [128, 1024])
    VH = sb("v_by_pair", [128, PAIRS, NBLK, 16])
    QF, KF = sb("q_full", [128, 512]), sb("k_full", [128, 512])
    QP, KP = sb("q_hi_lo", [128, 2, 2, 512]), sb("k_hi_lo", [128, 2, 2, 512])
    ST, MV = sb("ln_stats", [128, 4, 6]), sb("ln_mv", [128, 4, 2])
    VE, RSTD, MHALF = sb("ln_ve", [128, 4]), sb("ln_rstd", [128, 4]), sb("minus_half", [128, 4])
    QO, KO = sb("q_operand", [128, 3, 2, S], F32R), sb("k_operand", [128, 3, 2, S], F32R)
    TT = sb("bias_tables", [128, 3, 2, 3, 160], F32R)
    VB = sb("v_operand", [128, 3, 2, NBLK, 32])
    P = sb("probs", [128, 2, 2, S])
    SC = sb("band_scores", [128, 2, 160])
    MX = sb("max_parts", [128, 3, 2, NBLK, 3])
    M, MHL, MR = sb("row_max", [128, 2, NBLK]), sb("max_hi_lo", [128, 2, 2, NBLK]), sb("max_rows", [32, 128])
    CT, RC = sb("context_T", [128, 512]), sb("inv_sum", [128, 4, 4])

    PA = [pb(f"psA{n}", [128, S]) for n in range(2)]
    PB = [pb(f"psB{n}", [128, 512]) for n in range(2)]
    PV, PM = pb("psV", [128, 512]), pb("psM", [128, 512])

    names = ("w_in zero_ready half_ready x_ve x_rstd xn_ready xt_psum xt_ready q_psum k_psum v_psum qk_read v_read "
             "qk_split w_psum w_ready w_out step_out rows_ready flip_ready vb_zero vb_ready a_ready a_used "
             "b_ready exp_done pv_done evac_done max_parts max_psum max_rows max_out max_in ctx_psum ctx_used "
             "zeroed m_step r_step own_v").split()
    s = {n: sem(n) for n in names}
    x_in = [sem(f"x_in{n}") for n in range(4)]
    qk_out = [sem(f"qk_out{n}") for n in range(2)]
    ops_in = [sem(f"ops_in{n}") for n in range(3)]
    LOADS = 11
    AHEAD = 5

    x_v = x.rearrange("b (n p) d -> p (b n) d", p=128)
    LD_rows = LD.rearrange("h r t -> (h r t)").rearrange("(c p z) -> c p z", c=4, p=128)
    qd = QD.rearrange("a (n h d) t -> a d n h t", h=2, d=DH)
    kd = KD.rearrange("a (n h d) t -> a d n h t", h=2, d=DH)
    ld = LD.rearrange("(n h) r t -> r n h t", h=2)

    def steady(eng, do_pair):
        do_pair(Pair(0, 0), first=True)
        with eng.Fori(0, 4) as i:
            for r in range(1, 4):
                do_pair(Pair(i, r))
        do_pair(Pair(0, 13))
        do_pair(Pair(0, 14), left=1)
        do_pair(Pair(0, 15), left=0)

    block = ctx.enter_context(nc.Block())

    @block.sync
    def _(sp):
        for c in range(4):
            sp.dma_start(X[:, 4 * c:4 * c + 4, :], x_v[:, 4 * c:4 * c + 4, :]).then_inc(x_in[c], 16)
        for w, d in ((ID, ident_d), (WQ, Wq), (WK, Wk), (WV, Wv), (SEL, sel_d), (REL[:, 0:H], rel),
                     (REL[:, H:2 * H], rel), (FLIP, flip_d), (ROWS[32:48, :], rows_d),
                     (BQ, bq.rearrange("(p o) -> p o", o=1)), (BK, bk.rearrange("(p o) -> p o", o=1)),
                     (BV, bv.partition_broadcast(128))):
            sp.dma_start(w[:, :], d).then_inc(s["w_in"], 16)
        for dst, src in later_loads:
            sp.dma_start(dst, src).then_inc(loaded, 16)
        sp.wait_ge(s["zero_ready"], 1)
        for c in range(4):
            sp.dma_start(LD_rows[c], ZERO[:]).then_inc(s["step_out"], 16)
        sp.wait_ge(s["w_ready"], 3)
        sp.dma_start(WD[:], W3[:]).then_inc(s["w_out"], 16)
        sp.wait_ge(s["step_out"], 64)
        for r in range(1, NBLK):
            sp.dma_start(LD[:, 2 * (r - 1):2 * r, 128 * r:128 * r + 128],
                         W3[:, 1:3, STEP:STEP + 128]).then_inc(s["step_out"], 16)
        for c in range(4):
            b, half = c // 2, c % 2
            sp.wait_ge(s["qk_split"], 4 * (c + 1))
            for dst, src in ((QD, QP), (KD, KP)):
                for part in range(2):
                    sp.dma_start(dst[part, b * D:b * D + D, half * 512:half * 512 + 512],
                                 src[:, c % 2, part, :]).then_inc(qk_out[c % 2], 16)

        def load(p):
            q, k = QO[:, p.set, :, :].bitcast(F32), KO[:, p.set, :, :].bitcast(F32)
            one = bass.ds(p.n, 1)
            for n, (qpart, kpart) in enumerate(((0, 0), (0, 1), (1, 0), (1, 1))):
                rows = slice(DH * n, DH * n + DH)
                sp.dma_start(q[rows], qd[qpart][:, one].rearrange("d o h t -> d (o h) t")).then_inc(ops_in[p.set], 16)
                sp.dma_start(k[rows], kd[kpart][:, one].rearrange("d o h t -> d (o h) t")).then_inc(ops_in[p.set], 16)
            sp.dma_start(q[ROW_STEP:ROW_STEP + 16], ld[:, one].rearrange("r o h t -> r (o h) t")
                         ).then_inc(ops_in[p.set], 16)
            t = TT[:, p.set, :, :, :].bitcast(F32).rearrange("p h a c -> p (h a) c")
            for at, seg, n in ((0, DIAG, 128), (128, EDGE, 32)):
                sp.dma_start(t[:, :, at:at + n], bass.AP(WD.tensor, p.n * (2 * 3 * WCOLS) + seg,
                                                         [[1, 128], [WCOLS, 6], [1, n]])).then_inc(ops_in[p.set], 16)

        def maxima(p):
            sp.wait_ge(s["max_rows"], p.n + 1)
            sp.dma_start(MD.rearrange("n a h (t q) -> n (a h t) q", q=128)[bass.ds(p.n, 1)]
                         .rearrange("o r q -> (o r) q"), MR[:]).then_inc(s["max_out"], 16)
            sp.wait_ge(s["max_out"], p.n * 16 + 16)
            sp.dma_start(QO[ROW_MAX:ROW_MAX + 2, p.set, :, :].bitcast(F32),
                         MD.rearrange("n a h t -> a n h t")[:, bass.ds(p.n, 1)].rearrange("a o h t -> a (o h) t")
                         ).then_inc(s["max_in"], 16)

        for out in qk_out:
            sp.wait_ge(out, 16 * 8)
        sp.wait_ge(s["w_out"], 16)
        sp.wait_ge(s["step_out"], 16 * (4 + 7))
        sp.wait_ge(s["rows_ready"], 3)
        load(Pair(0, 0))
        load(Pair(0, 1))
        maxima(Pair(0, 0))

        def do_pair(p, first=False, left=2):
            if left == 2:
                if not first:
                    sp.wait_ge(s["b_ready"], p.n * 32)
                load(p + 2)
            if left:
                maxima(p + 1)

        steady(sp, do_pair)

    @block.gpsimd
    def _(pool):
        pool.memset(MHALF[:], -0.5).then_inc(s["half_ready"], 1)
        pool.memset(ZERO[:], 0.0).then_inc(s["zero_ready"], 1)
        pool.wait_ge(s["half_ready"], 1)
        for c in range(4):
            pool.wait_ge(s["x_ve"], c + 1)
            pool.tensor_tensor(RSTD[:], VE[:], MHALF[:], ALU.pow).then_inc(s["x_rstd"], 1)
            if c == 0:
                pool.memset(QO[:].bitcast(U32), 0).then_inc(s["zeroed"], 1)
                pool.memset(KO[:].bitcast(U32), 0).then_inc(s["zeroed"], 1)
        pool.memset(VB[:], 0.0).then_inc(s["vb_zero"], 1)
        pool.wait_ge(s["vb_zero"], 1)
        pool.memset(VB[:, :, :, :, DH:DH + 1], 1.0).then_inc(s["vb_zero"], 1)
        pool.wait_ge(s["v_read"], 4)
        pool.wait_ge(s["vb_zero"], 2)

        def values(p):
            for a in range(2):
                pool.tensor_copy(VB[:, p.set, a, :, 0:DH],
                                 VH[:, bass.ds(p.n, 1), :, a * DH:a * DH + DH].rearrange("p o n c -> p (o n) c")
                                 ).then_inc(s["vb_ready"], 1)

        values(Pair(0, 0))

        def do_pair(p, first=False, left=2):
            if left:
                if not first:
                    pool.wait_ge(s["pv_done"], (p.n - 1) * NBLK + 1)
                values(p + 1)

        steady(pool, do_pair)

    @block.scalar
    def _(act):
        for c in range(4):
            act.wait_ge(s["xt_psum"], c + 1)
            nc.scalar.copy(XT[:, 512 * c:512 * c + 512], PM[:]).then_inc(s["xt_ready"], 1)
            if c == 0:
                act.wait_ge(s["w_psum"], 1)
                nc.scalar.copy(W3[:, 0, :], PA[0][0:2 * H, 0:WCOLS]).then_inc(s["w_ready"], 1)

        def max_copy(p):
            act.wait_ge(s["max_psum"], p.n + 1)
            act.wait_ge(s["max_out"], p.n * 16)
            nc.scalar.copy(MR[:], PM[0:32, 0:128]).then_inc(s["max_rows"], 1)

        def evacuate(p):
            act.wait_ge(s["pv_done"], p.n * NBLK + NBLK)
            nc.scalar.copy(CT[:], PV[:]).then_inc(s["evac_done"], 1)

        max_copy(Pair(0, 0))

        def do_pair(p, first=False, left=2):
            for j in range(2 * NBLK):
                kb, a = j // 2, j % 2
                for half in range(2):
                    act.wait_ge(s["b_ready"], p.n * 32 + (2 * j + half + 1))
                    if half == 0 and a == 0 and not (first and kb < 2):
                        act.wait_ge(s["pv_done"], p.n * NBLK + (kb - 1))
                    nc.scalar.activation(P[:, kb % 2, a, half * 512:half * 512 + 512], PB[half][:],
                                         ACT.Exp).then_inc(s["exp_done"], 1)
                if j == 1 and not first:
                    evacuate(p + -1)
                if j == 2 * NBLK - AHEAD + 1 and left:
                    max_copy(p + 1)

        steady(act, do_pair)
        evacuate(Pair(0, 15))

    @block.tensor
    def _(pe):
        for c in range(4):
            pe.wait_ge(s["xn_ready"], 4 * c + 4)
            if c == 0:
                pe.wait_ge(s["w_in"], 16 * 12)
            else:
                pe.wait_ge(s["xt_ready"], c)
            for n in range(4):
                ins = nc.tensor.transpose(PM[:, 128 * n:128 * n + 128], XN[:, c % 2, n, :], ID[:])
            ins.then_inc(s["xt_psum"], 1)
            pe.wait_ge(s["xt_ready"], c + 1)
            if c:
                pe.wait_ge(s["qk_read"], 2 * c)
            xt = XT[:, 512 * c:512 * c + 512]
            nc.tensor.matmul(PB[0][:], WQ[:], xt, start=True, stop=True).then_inc(s["q_psum"], 1)
            nc.tensor.matmul(PB[1][:], WK[:], xt, start=True, stop=True).then_inc(s["k_psum"], 1)
            if c:
                pe.wait_ge(s["v_read"], c)
            for n in range(4):
                ins = nc.tensor.matmul(PV[:, 128 * n:128 * n + 128], xt[:, 128 * n:128 * n + 128], WV[:],
                                       start=True, stop=True)
            ins.then_inc(s["v_psum"], 1)
            if c == 0:
                for at in (0, 512):
                    end = min(at + 512, WCOLS)
                    ins = nc.tensor.matmul(PA[0][0:2 * H, at:end], REL[:], SEL[:, at:end], start=True, stop=True)
                ins.then_inc(s["w_psum"], 1)

        def scores(p, t):
            a, qb = t // NBLK, t % NBLK
            if t == 0:
                pe.wait_ge(ops_in[p.set], p.use * (16 * LOADS) + 16 * LOADS)
            if t > 1 or p.r > 0:
                pe.wait_ge(s["a_used"], p.n * 16 + (t - 1))
            for half in range(2):
                ins = nc.tensor.matmul(PA[t % 2][:, half * 512:half * 512 + 512],
                                       QO[:, p.set, a, 128 * qb:128 * qb + 128],
                                       KO[:, p.set, a, half * 512:half * 512 + 512], start=True, stop=True)
            ins.then_inc(s["a_ready"], 1)

        def scores_T(p, j, half, first):
            kb, a = j // 2, j % 2
            n = 2 * j + half
            if not (first and n < 2):
                pe.wait_ge(s["exp_done"], p.n * 32 + (n - 1))
            lo, hi = half * 512, half * 512 + 512
            c0, c1 = max(lo, 128 * kb), min(hi, 128 * kb + 160)
            ins = nc.tensor.matmul(PB[half][:], KO[:, p.set, a, 128 * kb:128 * kb + 128], QO[:, p.set, a, lo:hi],
                                   start=True, stop=c0 >= c1)
            if c0 < c1:
                for part in (1, 2):
                    ins = nc.tensor.matmul(PB[half][:, c0 - lo:c1 - lo], FLIPR[:],
                                           TT[:, p.set, a, part, c0 - 128 * kb:c1 - 128 * kb],
                                           start=False, stop=part == 2)
            ins.then_inc(s["b_ready"], 1)

        def values(p, kb):
            pe.wait_ge(s["exp_done"], p.n * 32 + (4 * kb + 4))
            if kb == 0:
                pe.wait_ge(s["vb_ready"], p.n * 2 + 2)
                if p.r:
                    pe.wait_ge(s["evac_done"], p.n)
            for a in range(2):
                for half in range(2):
                    g = 32 * (2 * a + half)
                    ins = nc.tensor.matmul(PV[g:g + 32, :], VB[:, p.set, a, kb, :],
                                           P[:, kb % 2, a, half * 512:half * 512 + 512],
                                           start=kb == 0, stop=kb == NBLK - 1, tile_position=(0, g))
            ins.then_inc(s["pv_done"], 1)

        def max_transpose(p):
            pe.wait_ge(s["max_parts"], p.n + 1)
            if p.r > 1:
                pe.wait_ge(s["ctx_used"], p.n - 1)
            nc.tensor.transpose(PM[0:32, 0:128], MHL[:].rearrange("p a h t -> p (a h t)"), ID[:]
                                ).then_inc(s["max_psum"], 1)

        def context_transpose(p):
            pe.wait_ge(s["evac_done"], p.n + 1)
            if p.r < PAIRS - 1:
                pe.wait_ge(s["max_rows"], p.n + 2)
            else:
                pe.wait_ge(s["ctx_used"], p.n)
            for c in range(4):
                ins = nc.tensor.transpose(PM[:, 128 * c:128 * c + 128], CT[:, 128 * c:128 * c + 128], ID[:])
            ins.then_inc(s["ctx_psum"], 1)

        pe.wait_ge(s["rows_ready"], 3)
        pe.wait_ge(s["flip_ready"], 1)
        pe.wait_ge(s["qk_read"], 8)
        pe.wait_ge(s["v_read"], 4)
        pe.wait_ge(s["w_ready"], 3)
        for t in range(16):
            scores(Pair(0, 0), t)
        for t in range(AHEAD):
            scores(Pair(0, 1), t)
        max_transpose(Pair(0, 0))

        def do_pair(p, first=False, left=2):
            for j in range(2 * NBLK):
                t = j + AHEAD
                if t < 16 and left:
                    scores(p + 1, t)
                if t >= 16 and left == 2:
                    scores(p + 2, t - 16)
                if j == 0:
                    pe.wait_ge(s["max_in"], p.n * 16 + 16)
                for half in range(2):
                    scores_T(p, j, half, first)
                if j == 0 and not first:
                    values(p + -1, NBLK - 1)
                if j % 2 == 0 and j:
                    values(p, j // 2 - 1)
                if j == 3 and not first:
                    context_transpose(p + -1)
                if j == 2 * NBLK - AHEAD + 1 and left:
                    max_transpose(p + 1)

        steady(pe, do_pair)
        values(Pair(0, 15), NBLK - 1)
        context_transpose(Pair(0, 15))

    @block.vector
    def _(dve):
        own = Chain(dve, s["own_v"])
        own.mark(nc.vector.memset(MX[:], -3.0e38))
        for c in range(4):
            dve.wait_ge(x_in[c], 16)
            for n in range(4):
                own.mark(nc.vector.bn_stats(ST[:, n, :], X[:, 4 * c + n, :]))
            own.settle()
            for n in range(4):
                own.mark(nc.vector.bn_aggr(MV[:, n, :], ST[:, n, :]))
            own.settle()
            nc.vector.tensor_scalar(VE[:], MV[:, :, 1], EPS, None, ALU.add).then_inc(s["x_ve"], 1)
            dve.wait_ge(s["x_rstd"], c + 1)
            if c >= 2:
                dve.wait_ge(s["xt_psum"], c - 1)
            for n in range(4):
                nc.vector.tensor_scalar(XN[:, c % 2, n, :], X[:, 4 * c + n, :], MV[:, n, 0:1], RSTD[:, n:n + 1],
                                        ALU.subtract, ALU.mult).then_inc(s["xn_ready"], 1)
            if c == 0:
                dve.wait_ge(s["w_in"], 16 * 12)
                nc.vector.tensor_copy(FLIPR[:], FLIP[:]).then_inc(s["flip_ready"], 1)
            if c >= 2:
                dve.wait_ge(qk_out[c % 2], 64 * (c // 2))
            dve.wait_ge(s["q_psum"], c + 1)
            nc.vector.tensor_scalar(QF[:], PB[0][:], BQ[:, 0:1], DH ** -0.5, ALU.add, ALU.mult
                                    ).then_inc(s["qk_read"], 1)
            dve.wait_ge(s["k_psum"], c + 1)
            nc.vector.tensor_scalar(KF[:], PB[1][:], BK[:, 0:1], None, ALU.add).then_inc(s["qk_read"], 1)
            dve.wait_ge(s["qk_read"], 2 * c + 2)
            for full, parts in ((QF, QP), (KF, KP)):
                nc.vector.tensor_copy(parts[:, c % 2, 0, :].bitcast(F32R), full[:]).then_inc(s["qk_split"], 1)
            dve.wait_ge(s["qk_split"], 4 * c + 2)
            for full, parts in ((QF, QP), (KF, KP)):
                nc.vector.tensor_tensor(parts[:, c % 2, 1, :].bitcast(F32R), full[:], parts[:, c % 2, 0, :],
                                        ALU.subtract).then_inc(s["qk_split"], 1)
            dve.wait_ge(s["v_psum"], c + 1)
            for n in range(4):
                blk = 4 * (c % 2) + n
                ins = nc.vector.tensor_tensor(
                    VH[:, 8 * (c // 2):8 * (c // 2) + 8, blk, :],
                    PV[:, 128 * n:128 * n + 128].rearrange("p (m c) -> p m c", c=16),
                    BV[:].rearrange("p (m c) -> p m c", c=16), ALU.add)
            ins.then_inc(s["v_read"], 1)
            if c == 0:
                dve.wait_ge(s["w_ready"], 1)
                nc.vector.tensor_copy(W3[:, 1, :].bitcast(F32R), W3[:, 0, :]).then_inc(s["w_ready"], 1)
                dve.wait_ge(s["w_ready"], 2)
                nc.vector.tensor_tensor(W3[:, 2, :].bitcast(F32R), W3[:, 0, :], W3[:, 1, :], ALU.subtract
                                        ).then_inc(s["w_ready"], 1)
            if c == 1:
                dve.wait_ge(s["zeroed"], 2)
                for m in range(3):
                    nc.vector.tensor_copy(KO[32:48, m, :, :], ROWS[32:48, :].rearrange("r (o t) -> r o t", o=1)
                                          .to_broadcast([16, 2, S])).then_inc(s["rows_ready"], 1)

        def reversed_table(p, a, c0, c1):
            view = TT[:, p.set, a, 0, 159 - c0:160 - c0].bitcast(F32)
            return bass.AP(view.tensor, view.offset, [list(view.ap[0]), [-1, c1 - c0]])

        def tile_max(p, t):
            a, qb = t // NBLK, t % NBLK
            left, right = 128 * qb - BAND, 128 * qb + 128
            ps, mx = PA[t % 2], MX[:, p.set, a, qb, :]
            if t > 1 or p.r:
                dve.wait_ge(s["a_used"], p.n * 16 + (t - 1))
            dve.wait_ge(s["a_ready"], p.n * 16 + (t + 1))
            if qb:
                nc.vector.tensor_reduce(mx[:, 0:1], ps[:, 0:left], AX.X, ALU.max)
            if qb < NBLK - 1:
                nc.vector.tensor_reduce(mx[:, 2:3], ps[:, right:S], AX.X, ALU.max)
            c0 = max(left, 0)
            nc.vector.tensor_tensor_reduce(SC[:, t % 2, 0:right - c0], ps[:, c0:right],
                                           reversed_table(p, a, c0 - left, 160), 1.0, -3.0e38, ALU.add, ALU.max,
                                           mx[:, 1:2]).then_inc(s["a_used"], 1)

        def pair_max(p):
            dve.wait_ge(s["a_used"], p.n * 16 + 16)
            nc.vector.tensor_reduce(M[:], MX[:, p.set, :, :, :], AX.X, ALU.max).then_inc(s["m_step"], 1)
            if p.r:
                dve.wait_ge(s["max_psum"], p.n)
            dve.wait_ge(s["m_step"], p.n * 2 + 1)
            nc.vector.tensor_scalar(MHL[:, 0, :, :].bitcast(F32R), M[:], -1.0, None, ALU.mult
                                    ).then_inc(s["m_step"], 1)
            dve.wait_ge(s["m_step"], p.n * 2 + 2)
            nc.vector.scalar_tensor_tensor(MHL[:, 1, :, :].bitcast(F32R), M[:], -1.0, MHL[:, 0, :, :],
                                           ALU.mult, ALU.subtract).then_inc(s["max_parts"], 1)

        def context(p):
            view = PM[:].rearrange("p (c a h w) -> p a h c w", c=4, a=2, h=2)
            dve.wait_ge(s["ctx_psum"], p.n + 1)
            nc.vector.reciprocal(RC[:].rearrange("p c g -> p g c"),
                                 PM[:].rearrange("p (c g w) -> p g c w", c=4, g=4)[:, :, :, DH]
                                 ).then_inc(s["r_step"], 1)
            dve.wait_ge(s["r_step"], p.n + 1)
            for a in range(2):
                out = CTXH[:, bass.ds(p.n, 1), :, a * DH:a * DH + DH].rearrange("p o (h c) w -> p (o h) c w", h=2)
                inv = RC[:].rearrange("p c (a h o) -> p a h c o", a=2, o=1)[:, a].to_broadcast([128, 2, 4, DH])
                ins = nc.vector.tensor_tensor(out, view[:, a, :, :, 0:DH], inv, ALU.mult)
            ins.then_inc(s["ctx_used"], 1)

        own.settle()
        for t in range(16):
            if t == 0:
                dve.wait_ge(ops_in[0], 16 * LOADS)
            tile_max(Pair(0, 0), t)
        pair_max(Pair(0, 0))
        for t in range(AHEAD):
            if t == 0:
                dve.wait_ge(ops_in[1], 16 * LOADS)
            tile_max(Pair(0, 1), t)

        def do_pair(p, first=False, left=2):
            for j in range(2 * NBLK):
                t = j + AHEAD
                if t < 16 and left:
                    tile_max(p + 1, t)
                    if t == 15:
                        pair_max(p + 1)
                if t >= 16 and left == 2:
                    if t == 16:
                        q = p + 2
                        dve.wait_ge(ops_in[q.set], q.use * (16 * LOADS) + 16 * LOADS)
                    tile_max(p + 2, t - 16)
                if j == 4 and not first:
                    context(p + -1)

        steady(dve, do_pair)
        context(Pair(0, 15))


FF = 512
NE, HID = 8, 352
MROWS = (128, 128, 96)
CH = 4
PARTS = 3 * NE


def tail_weights(nc, ctx, w):
    def sb(name, shape):
        return ctx.enter_context(nc.sbuf_tensor("wt_" + name, shape, F32))

    t = {"r": sb("r", [D, D]), "k": sb("k", [D, D]), "v": sb("v", [D, D]),
         "mu": sb("mu", [D, 2]), "rows": sb("rows", [128, 6, D]), "l1": sb("l1", [D, FF]), "b1": sb("b1", [128, 4]),
         "l2": sb("l2", [128, 4, D]), "gate": sb("gate", [D, NE]), "iota": sb("iota", [128, NE]),
         "w1": sb("w1", [D, NE, HID]), "w3": sb("w3", [D, NE, HID]), "w2": sb("w2", [128, NE, 3, D])}
    loads = [(t["r"][:], w["W_r"]), (t["k"][:], w["W_k"]), (t["v"][:], w["W_v"]),
             (t["mu"][:, 0:1], w["mu_r"].rearrange("(p o) -> p o", o=1)),
             (t["mu"][:, 1:2], w["mu_k"].rearrange("(p o) -> p o", o=1)),
             (t["l1"][:], w["l1_w1"]), (t["b1"][:], w["b1"]),
             (t["l2"][:], w["l1_w2"].rearrange("(m p) d -> p m d", p=128)),
             (t["gate"][:], w["gate_w"]), (t["iota"][:], w["iota"].partition_broadcast(128)),
             (t["w1"][:], w["w1"]), (t["w3"][:], w["w3"])]
    for n, name in enumerate(("lmlg", "theta", "init", "ln_w", "ln_b", "b2")):
        loads.append((t["rows"][:, n, :], w[name].partition_broadcast(128)))
    for m, rows in enumerate(MROWS):
        loads.append((t["w2"][0:rows, :, m, :], w["w2"][:, 128 * m:128 * m + rows, :].rearrange("e p d -> p e d")))
    return t, loads


def tail_block(nc, ctx, t, n_loads, loaded, ident, X, CTXH, out):
    def sb(name, shape, dt=F32):
        return ctx.enter_context(nc.sbuf_tensor("t_" + name, shape, dt))

    def pb(name):
        return ctx.enter_context(nc.psum_tensor(name, [128, 512], F32))

    names = ("own_c own_p own_r own_g gamma angle cosine gap gap_exp ve rstd xn1 t1 xnt mixed r_psum k_psum sig relu ka v_psum y_done acc_done "
             "h2 t2 h2t up_hid hid l2_psum x3 xm t3 xmt logits up_u up_v silu hm down added stored half").split()
    s = {n: ctx.enter_context(nc.semaphore("t_" + n)) for n in names}

    X1, X2, X3, XN = sb("x1", [128, 4, D]), sb("x2", [128, 4, D]), sb("x3", [128, 4, D]), sb("xn", [128, 4, D])
    ST, MV, VE, RSTD = sb("st", [128, 4, 6]), sb("mv", [128, 4, 5]), sb("ve", [128, 4]), sb("rstd", [128, 4])
    MHALF, MEAN, HOLD = sb("mhalf", [128, 4]), sb("mean", [128, 4]), sb("hold", [128, 2])
    XNT = sb("xnt", [128, 2, 257])
    MU1 = sb("mu1", [128, 2])
    TMP, XR, XK = sb("tmp", [128, 2, 256]), sb("xr", [128, 2, 256]), sb("xk", [128, 2, 256])
    KR, KA, RS = sb("kr", [128, 512]), sb("ka", [128, 512]), sb("rs", [128, 4, D])
    A, HH, U, Y, ACC = (sb(n, [128, 4, D]) for n in ("a", "h", "u", "y", "acc"))
    H2T, HIDT, XMT = sb("h2t", [128, 512]), sb("hidt", [128, 4, 512]), sb("xmt", [128, 512])
    CR, CI, CI2 = sb("cr", [128, D]), sb("ci", [128, D]), sb("ci2", [128, D])
    W1, W2, W4, W5 = (sb(f"work{n}", [128, D]) for n in range(4))
    LG, M8, I8, IF = sb("lg", [128, 4, 8]), sb("m8", [128, 4, 8]), sb("i8", [128, 4, 8], U32), sb("if", [128, 4, 2])
    DL, EX, SM, RW, EW = (sb(n, [128, 4]) for n in ("dl", "ex", "sm", "rw", "ew"))
    E1, E2, G = sb("e1", [128, 4, NE]), sb("e2", [128, 4, NE]), sb("g", [128, 4, NE])
    SU, HM = sb("su", [128, 2, 512]), sb("hm", [128, 2, 3, 512])
    OUT = sb("out", [128, 4, D])
    PU, PVV, PY = [pb("pu0"), pb("pu1")], [pb("pv0"), pb("pv1")], [pb("py0"), pb("py1")]
    R0, R1 = pb("pr0"), pb("pr1")
    LMLG, THETA, INIT, LNW, LNB, B2 = (t["rows"][:, n, :] for n in range(6))

    def wide(row):
        return row.rearrange("p (o d) -> p o d", o=1).to_broadcast([128, 4, D])

    def wide2(row):
        return row.rearrange("p (o d) -> p o d", o=1).to_broadcast([128, 2, D])

    NORMS = 5
    out_v = out.rearrange("b (n p) d -> p b n d", p=128)
    block = ctx.enter_context(nc.Block())

    def run(eng, before, part, after):
        for k in range(PARTS):
            part(-1, k, False, True)
        before(0)
        with eng.Fori(0, CH - 1) as c:
            for k in range(PARTS):
                part(c, k, True, True)
            after(c)
            before(c + 1)
        for k in range(PARTS):
            part(CH - 1, k, True, False)
        after(CH - 1)

    @block.sync
    def _(sp):
        with sp.Fori(0, CH) as c:
            sp.wait_ge(s["added"], c * NE + (NE + 2))
            for b in range(B):
                sp.dma_start(out_v[:, b, bass.ds(2 * c, 2), :], OUT[:, 2 * b:2 * b + 2, :]).then_inc(s["stored"], 16)
        sp.wait_ge(s["stored"], CH * 32 + 16)

    @block.gpsimd
    def _(pool):
        pool.memset(MHALF[:], -0.5).then_inc(s["half"], 1)
        pool.wait_ge(s["half"], 1)

        def rstd(c, n):
            pool.wait_ge(s["ve"], c * NORMS + (n + 1))
            pool.tensor_tensor(RSTD[:], VE[:], MHALF[:], ALU.pow).then_inc(s["rstd"], 1)

        def chunk(c):
            for n in range(4):
                rstd(c, n)
            pool.wait_ge(s["y_done"], c + 1)
            pool.tensor_tensor(ACC[:], X2[:], Y[:], ALU.add).then_inc(s["own_p"], 1)
            pool.wait_ge(s["own_p"], c + 1)
            pool.tensor_tensor(ACC[:], ACC[:], wide(B2), ALU.add).then_inc(s["acc_done"], 1)
            rstd(c, 4)

        with pool.Fori(0, CH) as c:
            chunk(c)

    @block.scalar
    def _(act):
        act.wait_ge(loaded, 16 * n_loads)
        nc.scalar.activation(W1[:], LMLG, ACT.Exp).then_inc(s["gamma"], 1)
        act.wait_ge(s["gamma"], 1)
        nc.scalar.activation(W2[:], W1[:], ACT.Exp, scale=-1.0).then_inc(s["gamma"], 1)
        act.wait_ge(s["angle"], 1)
        nc.scalar.activation(W5[:], W4[:], ACT.Sin, scale=float(2 * np.pi)).then_inc(s["cosine"], 1)

        def part(c, k, moe, pre):
            if moe:
                n = c * PARTS + (k + 1)
                rows = MROWS[k % 3]
                act.wait_ge(s["up_u"], n)
                act.wait_ge(s["hm"], n)
                nc.scalar.activation(SU[0:rows, k % 2, :], PU[k % 2][0:rows, :], ACT.Silu).then_inc(s["silu"], 1)
            if pre:
                d = c + 1
                if k == 2:
                    act.wait_ge(s["t1"], d + 1)
                    act.wait_ge(s["mixed"], d)
                    nc.scalar.copy(XNT[:, :, 1:257], R0[:].rearrange("p (b t) -> p b t", b=2)).then_inc(s["xnt"], 1)
                if k == 4:
                    act.wait_ge(s["k_psum"], d + 1)
                    nc.scalar.activation(KR[:], R0[:], ACT.Relu).then_inc(s["relu"], 1)
                    act.wait_ge(s["r_psum"], d + 1)
                    nc.scalar.activation(RS[:].rearrange("p g d -> p (g d)"), R1[:], ACT.Sigmoid).then_inc(s["sig"], 1)
                if k == 12:
                    act.wait_ge(s["t2"], d + 1)
                    nc.scalar.copy(H2T[:], R1[:]).then_inc(s["h2t"], 1)
                if k in (13, 15):
                    for m in (k - 13, k - 12):
                        act.wait_ge(s["up_hid"], d * 4 + (m + 1))
                        if m == 0:
                            act.wait_ge(s["l2_psum"], d)
                        nc.scalar.activation(HIDT[:, m, :], (R0, R1)[m % 2][:], ACT.Silu, bias=t["b1"][:, m:m + 1]
                                             ).then_inc(s["hid"], 1)

        def to_experts(c):
            act.wait_ge(s["t3"], c + 1)
            nc.scalar.copy(XMT[:], R1[:]).then_inc(s["xmt"], 1)
            act.wait_ge(s["gap"], c + 1)
            nc.scalar.activation(EX[:], DL[:], ACT.Exp).then_inc(s["gap_exp"], 1)

        act.sem_inc(s["silu"], 2)
        run(act, to_experts, part, lambda c: None)

    @block.tensor
    def _(pe):
        pe.wait_ge(loaded, 16 * n_loads)

        def transpose4(src, dst, done):
            for g in range(4):
                ins = nc.tensor.transpose(dst[:, 128 * g:128 * g + 128], src[:, g, :], ident[:])
            ins.then_inc(done, 1)

        def down(c, e):
            pe.wait_ge(s["hm"], c * PARTS + (3 * e + 3 + 2))
            pe.wait_ge(s["added"], c * NE + (e + 1))
            for g in range(4):
                for m, rows in enumerate(MROWS):
                    ins = nc.tensor.matmul(PY[e % 2][:, 128 * g:128 * g + 128],
                                           HM[0:rows, e % 2, m, 128 * g:128 * g + 128], t["w2"][0:rows, e, m, :],
                                           start=m == 0, stop=m == 2)
            ins.then_inc(s["down"], 1)

        def part(c, k, moe, pre):
            e, m = k // 3, k % 3
            if moe:
                n = c * PARTS + (k + 1)
                rows = MROWS[m]
                if k == 0:
                    pe.wait_ge(s["xmt"], c + 1)
                pe.wait_ge(s["silu"], n)
                nc.tensor.matmul(PU[k % 2][0:rows, :], t["w1"][:, e, 128 * m:128 * m + rows], XMT[:],
                                 start=True, stop=True).then_inc(s["up_u"], 1)
                pe.wait_ge(s["hm"], n)
                nc.tensor.matmul(PVV[k % 2][0:rows, :], t["w3"][:, e, 128 * m:128 * m + rows], XMT[:],
                                 start=True, stop=True).then_inc(s["up_v"], 1)
                if m == 2 and e:
                    down(c, e - 1)
            if pre:
                d = c + 1
                if k == 2:
                    pe.wait_ge(s["xn1"], d + 1)
                    transpose4(XN, R0, s["t1"])
                if k == 4:
                    pe.wait_ge(s["mixed"], d + 1)
                    nc.tensor.matmul(R0[:], t["k"][:], XK[:].rearrange("p b t -> p (b t)"), start=True, stop=True
                                     ).then_inc(s["k_psum"], 1)
                    xr = XR[:].rearrange("p b t -> p (b t)")
                    for g in range(4):
                        ins = nc.tensor.matmul(R1[:, 128 * g:128 * g + 128], xr[:, 128 * g:128 * g + 128], t["r"][:],
                                               start=True, stop=True)
                    ins.then_inc(s["r_psum"], 1)
                if k == 6:
                    pe.wait_ge(s["ka"], d + 1)
                    for g in range(4):
                        ins = nc.tensor.matmul(R0[:, 128 * g:128 * g + 128], KA[:, 128 * g:128 * g + 128], t["v"][:],
                                               start=True, stop=True)
                    ins.then_inc(s["v_psum"], 1)
                if k == 12:
                    pe.wait_ge(s["sig"], d + 1)
                    pe.wait_ge(s["h2"], d + 1)
                    transpose4(XN, R1, s["t2"])
                if k in (13, 15):
                    for m in (k - 13, k - 12):
                        if m == 0:
                            pe.wait_ge(s["h2t"], d + 1)
                        if m >= 2:
                            pe.wait_ge(s["hid"], d * 4 + (m - 1))
                        nc.tensor.matmul((R0, R1)[m % 2][:], t["l1"][:, 128 * m:128 * m + 128], H2T[:],
                                         start=True, stop=True).then_inc(s["up_hid"], 1)
                if k == 17:
                    pe.wait_ge(s["hid"], d * 4 + 4)
                    for g in range(4):
                        for m in range(4):
                            ins = nc.tensor.matmul(R0[:, 128 * g:128 * g + 128], HIDT[:, m, 128 * g:128 * g + 128],
                                                   t["l2"][:, m, :], start=m == 0, stop=m == 3)
                    ins.then_inc(s["l2_psum"], 1)
                if k == 23:
                    pe.wait_ge(s["xm"], d + 1)
                    transpose4(XN, R1, s["t3"])

        def after(c):
            down(c, NE - 1)

        def to_experts(c):
            pe.wait_ge(s["xmt"], c + 1)
            for g in range(4):
                ins = nc.tensor.matmul(R0[:, 8 * g:8 * g + 8], XMT[:, 128 * g:128 * g + 128], t["gate"][:],
                                       start=True, stop=True)
            ins.then_inc(s["logits"], 1)

        run(pe, to_experts, part, after)

    @block.vector
    def _(dve):
        V = nc.vector
        dve.sem_inc(s["hm"], 2)
        dve.sem_inc(s["added"], 2)
        dve.sem_inc(s["stored"], 16)
        dve.wait_ge(loaded, 16 * n_loads)
        own = Chain(dve, s["own_c"])
        own.mark(V.tensor_scalar(W4[:], THETA, float(0.5 / np.pi), 0.25, ALU.mult, ALU.add))
        own.mark(V.tensor_scalar(MU1[:], t["mu"][:], -1.0, 1.0, ALU.mult, ALU.add))
        own.mark(V.memset(XNT[:, :, 0:1], 0.0))
        own.settle()
        ROUND = float(1.5 * 2 ** 23)
        own.mark(V.tensor_scalar(W5[:], W4[:], ROUND, ROUND, ALU.add, ALU.subtract))
        own.settle()
        own.mark(V.tensor_tensor(W5[:], W4[:], W5[:], ALU.subtract))
        own.settle()
        V.tensor_scalar(W4[:], W5[:], 0.4999999, -0.4999999, ALU.min, ALU.max).then_inc(s["angle"], 1)
        dve.wait_ge(s["gamma"], 2)
        dve.wait_ge(s["cosine"], 1)
        own.mark(V.tensor_tensor(CR[:], W2[:], W5[:], ALU.mult))
        own.mark(V.tensor_tensor(W1[:], W2[:], W2[:], ALU.mult))
        own.mark(V.tensor_tensor(W4[:], W5[:], W5[:], ALU.mult))
        own.settle()
        own.mark(V.tensor_tensor(CI[:], CR[:], INIT, ALU.mult))
        own.mark(V.tensor_scalar(W2[:], W4[:], 2.0, -1.0, ALU.mult, ALU.add))
        own.mark(V.tensor_tensor(W5[:], W1[:], INIT, ALU.mult))
        own.settle()
        own.mark(V.tensor_tensor(CI2[:], W5[:], W2[:], ALU.mult))
        own.settle()

        PRE_MARKS, ROUTE_MARKS = 69, 18

        def stats(ch, src):
            for g in range(4):
                ch.mark(V.bn_stats(ST[:, g, :], src[:, g, :]))
            ch.settle()
            ch.mark(V.tensor_tensor(MV[:, :, 0], ST[:, :, 1], ST[:, :, 4], ALU.add))
            ch.mark(V.tensor_tensor(MV[:, :, 1], ST[:, :, 1], ST[:, :, 4], ALU.subtract))
            ch.mark(V.tensor_tensor(MV[:, :, 2], ST[:, :, 2], ST[:, :, 5], ALU.add))
            ch.settle()
            ch.mark(V.tensor_scalar(MEAN[:], MV[:, :, 0], 0.5, None, ALU.mult))
            ch.mark(V.scalar_tensor_tensor(MV[:, :, 3], MV[:, :, 1], 0.25, MV[:, :, 1], ALU.mult, ALU.mult))
            ch.mark(V.tensor_scalar(MV[:, :, 4], MV[:, :, 2], 1.0 / D, EPS, ALU.mult, ALU.add))
            ch.settle()
            V.tensor_tensor(VE[:], MV[:, :, 3], MV[:, :, 4], ALU.add).then_inc(s["ve"], 1)

        def normed(c, n, src, dst):
            dve.wait_ge(s["rstd"], c * NORMS + (n + 1))
            for g in range(4):
                ins = V.tensor_scalar(dst[:, g, :], src[:, g, :], MEAN[:, g:g + 1], RSTD[:, g:g + 1],
                                      ALU.subtract, ALU.mult)
            return ins

        pres = {}

        def pre_step(d, k):
            if k == 0:
                pres["ch"] = Chain(dve, s["own_r"], d * PRE_MARKS)
            ch = pres["ch"]
            if k == 0:
                for b in range(B):
                    x = X[:, bass.ds(NBLK * b + 2 * d, 2), :].rearrange("p n (h w) -> p n h w", w=16)
                    a = CTXH[:, NBLK * b:NBLK * b + 8, bass.ds(2 * d, 2), :].rearrange("p h n w -> p n h w")
                    ch.mark(V.tensor_tensor(X1[:, 2 * b:2 * b + 2, :].rearrange("p n (h w) -> p n h w", w=16),
                                            x, a, ALU.add))
                ch.settle()
                stats(ch, X1)
            if k == 1:
                dve.wait_ge(s["t3"], d)
                normed(d, 0, X1, XN).then_inc(s["xn1"], 1)
            if k == 3:
                dve.wait_ge(s["xnt"], d + 1)
                dve.wait_ge(s["r_psum"], d)
                now, prev = XNT[:, :, 1:257], XNT[:, :, 0:256]
                for n, x in enumerate((XR, XK)):
                    ch.mark(V.tensor_scalar(x[:], prev, MU1[:, n:n + 1], None, ALU.mult))
                ch.settle()
                for n, x in enumerate((XR, XK)):
                    ch.mark(V.scalar_tensor_tensor(x[:], now, t["mu"][:, n:n + 1], x[:], ALU.mult, ALU.add))
                V.tensor_copy(XNT[:, :, 0:1], XNT[:, :, 256:257]).then_inc(s["mixed"], 1)
            if k == 5:
                dve.wait_ge(s["relu"], d + 1)
                V.tensor_tensor(KA[:], KR[:], KR[:], ALU.mult).then_inc(s["ka"], 1)
            if k == 7:
                dve.wait_ge(s["v_psum"], d + 1)
                dve.wait_ge(s["sig"], d + 1)
                ch.mark(V.tensor_tensor(U[:], RS[:], R0[:].rearrange("p (g d) -> p g d", g=4), ALU.mult))
                ch.settle()
                dve.wait_ge(s["acc_done"], d)
                ch.mark(V.tensor_tensor(X2[:], X1[:], U[:], ALU.add))
                ch.settle()
                stats(ch, X2)
            if k == 8:
                ch.mark(normed(d, 1, X2, A))
                ch.settle()
                stats(ch, A)
            if k == 9:
                ch.mark(normed(d, 2, A, HH))
                ch.settle()
                ch.mark(V.tensor_tensor(HH[:], HH[:], wide(LNW), ALU.mult))
                ch.settle()
                ch.mark(V.tensor_tensor(HH[:], HH[:], wide(LNB), ALU.add))
                ch.settle()
                h0, h1 = HH[:, 0:2, :], HH[:, 2:4, :]
                ch.mark(V.tensor_tensor(U[:, 0:2, :], h0, wide2(CI[:]), ALU.add))
                ch.mark(V.tensor_tensor(U[:, 2:4, :], h0, wide2(CR[:]), ALU.mult))
                ch.settle()
                ch.mark(V.tensor_tensor(U[:, 2:4, :], U[:, 2:4, :], wide2(CI2[:]), ALU.add))
                ch.settle()
                ch.mark(V.tensor_tensor(U[:, 2:4, :], U[:, 2:4, :], h1, ALU.add))
                ch.settle()
            if k == 10:
                ch.mark(V.tensor_tensor(Y[:], U[:], HH[:], ALU.mult))
                ch.settle()
                V.tensor_tensor(Y[:], Y[:], A[:], ALU.add).then_inc(s["y_done"], 1)
                dve.wait_ge(s["y_done"], d + 1)
                stats(ch, Y)
            if k == 11:
                ch.mark(normed(d, 3, Y, XN))
                ch.settle()
                ch.mark(V.tensor_tensor(XN[:], XN[:], wide(LNW), ALU.mult))
                ch.settle()
                V.tensor_tensor(XN[:], XN[:], wide(LNB), ALU.add).then_inc(s["h2"], 1)
            if k == 18:
                dve.wait_ge(s["l2_psum"], d + 1)
                dve.wait_ge(s["acc_done"], d + 1)
                V.tensor_tensor(X3[:], ACC[:], R0[:].rearrange("p (g d) -> p g d", g=4), ALU.add
                                ).then_inc(s["x3"], 1)
                dve.wait_ge(s["x3"], d + 1)
                stats(ch, X3)
            if k == 19:
                normed(d, 4, X3, XN).then_inc(s["xm"], 1)
            if k == 23:
                pres["n"] = ch.k

        def gates(c):
            ch = Chain(dve, s["own_g"], c * ROUTE_MARKS)
            dve.wait_ge(s["logits"], c + 1)
            ch.mark(V.tensor_copy(LG[:], R0[:, 0:32].rearrange("p (g e) -> p g e", g=4)))
            ch.settle()
            V.memset(HOLD[:, 0:1], 0.0)
            for g in range(4):
                ch.mark(V.max(M8[:, g, :], LG[:, g, :]))
            ch.settle()
            V.memset(HOLD[:, 1:2], 0.0)
            for g in range(4):
                ch.mark(V.max_index(I8[:, g, :], M8[:, g, :], LG[:, g, :]))
            V.tensor_tensor(DL[:], M8[:, :, 1], M8[:, :, 0], ALU.subtract).then_inc(s["gap"], 1)
            ch.settle()
            ch.mark(V.tensor_copy(IF[:], I8[:, :, 0:2]))
            ch.settle()
            iota = t["iota"][:].rearrange("p (o e) -> p o e", o=1).to_broadcast([128, 4, NE])
            for n, eq in enumerate((E1, E2)):
                ch.mark(V.tensor_tensor(eq[:], iota, IF[:, :, n:n + 1].to_broadcast([128, 4, NE]), ALU.is_equal))
            dve.wait_ge(s["gap_exp"], c + 1)
            ch.mark(V.tensor_scalar(SM[:], EX[:], 1.0, None, ALU.add))
            ch.settle()
            ch.mark(V.reciprocal(RW[:], SM[:]))
            ch.settle()
            ch.mark(V.tensor_tensor(EW[:], EX[:], RW[:], ALU.mult))
            ch.settle()
            for eq, w in ((E1, RW), (E2, EW)):
                ch.mark(V.tensor_tensor(eq[:], eq[:], w[:].rearrange("p (g o) -> p g o", o=1)
                                        .to_broadcast([128, 4, NE]), ALU.mult))
            ch.settle()
            ch.mark(V.tensor_tensor(G[:], E1[:], E2[:], ALU.add))
            ch.settle()
            assert ch.k == ROUTE_MARKS, ch.k

        def add_expert(c, e):
            dve.wait_ge(s["down"], c * NE + (e + 1))
            if e:
                dve.wait_ge(s["added"], c * NE + (e + 2))
            else:
                dve.wait_ge(s["stored"], c * 32 + 16)
            for g in range(4):
                ins = V.scalar_tensor_tensor(OUT[:, g, :], PY[e % 2][:, 128 * g:128 * g + 128], G[:, g, e:e + 1],
                                             (OUT if e else X3)[:, g, :], ALU.mult, ALU.add)
            ins.then_inc(s["added"], 1)

        def part(c, k, moe, pre):
            e, m = k // 3, k % 3
            if moe:
                n = c * PARTS + (k + 1)
                rows = MROWS[m]
                dve.wait_ge(s["silu"], n + 2)
                dve.wait_ge(s["up_v"], n)
                if m == 0 and e >= 2:
                    dve.wait_ge(s["down"], c * NE + (e - 1))
                V.tensor_tensor(HM[0:rows, e % 2, m, :], SU[0:rows, k % 2, :], PVV[k % 2][0:rows, :], ALU.mult
                                ).then_inc(s["hm"], 1)
                if m == 2 and e:
                    add_expert(c, e - 1)
            if pre:
                pre_step(c + 1, k)

        run(dve, gates, part, lambda c: add_expert(c, NE - 1))
        assert pres["n"] == PRE_MARKS, pres["n"]


def program(nc, a, out):
    ctx = ExitStack()
    with ctx:
        X = ctx.enter_context(nc.sbuf_tensor("x", [128, B * NBLK, D], F32))
        CTXH = ctx.enter_context(nc.sbuf_tensor("context", [128, PAIRS, NBLK, 16], F32))
        ID = ctx.enter_context(nc.sbuf_tensor("sb_ident", [128, 128], F32))
        loaded = ctx.enter_context(nc.semaphore("loaded"))
        weights, loads = tail_weights(nc, ctx, a)
        with ExitStack() as attn:
            attention_block(nc, attn, [a[n] for n in ("x", "Wq", "bq", "Wk", "bk", "Wv", "bv", "rel", "ident",
                                                      "flip", "sel", "rows")], X, CTXH, ID, loads, loaded)
        with ExitStack() as tail:
            tail_block(nc, tail, weights, len(loads), loaded, ID, X, CTXH, out)


def kernel(**inputs):
    import numpy as _np
    import concourse.bacc as _bacc
    from concourse import mybir as _mybir
    from concourse.bass_utils import run_bass_kernel_spmd as _run

    g = inputs
    arrays = {
        "x": g["L0_attn_hidden_states"], "Wq": g["L0_attn_Wq"], "bq": g["L0_attn_bq"], "Wk": g["L0_attn_Wk"],
        "bk": g["L0_attn_bk"], "Wv": g["L0_attn_Wv"], "bv": g["L0_attn_bv"], "rel": g["L0_attn_rel_bias"],
        "W_r": g["L0_ffn_W_r"].T, "W_k": g["L0_ffn_W_k"].T, "W_v": g["L0_ffn_W_v"].T,
        "mu_r": g["L0_ffn_mu_r"], "mu_k": g["L0_ffn_mu_k"],
        "lmlg": g["L1_attn_lmlg"], "theta": g["L1_attn_theta"], "init": g["L1_attn_last_conv_init"],
        "ln_w": g["L1_attn_ln_w"], "ln_b": g["L1_attn_ln_b"], "l1_w1": g["L1_attn_w1"], "b1": g["L1_attn_b1"].reshape(4, 128).T,
        "l1_w2": g["L1_attn_w2"], "b2": g["L1_attn_b2"],
        "gate_w": g["L1_ffn_gate_w"].T, "w1": g["L1_ffn_w1"].transpose(2, 0, 1),
        "w3": g["L1_ffn_w3"].transpose(2, 0, 1), "w2": g["L1_ffn_w2"].transpose(0, 2, 1),
        "ident": _np.eye(128, dtype=_np.float32), "flip": _np.eye(128, dtype=_np.float32)[::-1],
        "sel": bias_selectors(), "rows": step_rows(), "iota": _np.arange(NE, dtype=_np.float32),
    }
    arrays = {f"in_{n}": _np.ascontiguousarray(a) for n, a in arrays.items()}
    nc = _bacc.Bacc("TRN2", target_bir_lowering=False, num_devices=1)
    aps = {n[3:]: nc.dram_tensor(n, a.shape, _mybir.dt.from_np(a.dtype), kind="ExternalInput").ap()
           for n, a in arrays.items()}
    out = nc.dram_tensor("out", (B, S, D), F32, kind="ExternalOutput").ap()
    program(nc, aps, out)
    r = _run(nc, [arrays], core_ids=[0])
    return r.results[0]["out"]
```

```python
import concourse.bass as bass
from concourse import mybir
from concourse.alu_op_type import AluOpType as ALU
from contextlib import ExitStack
import numpy as np

F32 = mybir.dt.float32
F32R = mybir.dt.float32r
U32 = mybir.dt.uint32
ACT = mybir.ActivationFunctionType
AX = mybir.AxisListType

B, S, D = 2, 1024, 128
H = 16
DH = D // H
NB = 32
NBLK = S // 128
PAIRS = B * H // 2
BAND = 32
EPS = 1e-5

DIAG, EDGE, STEP = 0, 256, 416
WCOLS = 544
ROW_STEP = 32
ROW_MAX = 46


def buckets(n):
    n = np.maximum(n, 0)
    large = 16 + (np.log(np.maximum(n, 1).astype(np.float32) / np.float32(16)) / np.float32(np.log(2.0))
                  * np.float32(16)).astype(np.int32)
    return np.where(n < 16, n, np.minimum(large, NB - 1))


def bias_selectors():
    sel = np.zeros((NB, WCOLS), np.float32)
    for at, distances, base in ((DIAG, range(-127, 128), 0), (EDGE, range(1, 160), NB - 1), (STEP, [BAND] * 128, 0)):
        for c, n in enumerate(distances):
            sel[buckets(np.array(n)), at + c] += 1
            sel[base, at + c] -= 1
    return sel


def step_rows():
    rows = np.zeros((16, S), np.float32)
    for r in range(1, NBLK):
        rows[2 * (r - 1):2 * r, :128 * r] = 1
    rows[14:16] = 1
    return rows


class Pair:

    def __init__(self, turn, r):
        self.turn, self.r = turn, r
        self.set = r % 3
        self.use = r // 3 + turn

    def __add__(self, n):
        return Pair(self.turn, self.r + n)

    @property
    def n(self):
        return self.turn * 3 + self.r


class Chain:

    def __init__(self, eng, sem, base=0):
        self.eng, self.sem, self.base, self.k = eng, sem, base, 0

    def mark(self, ins):
        self.k += 1
        return ins.then_inc(self.sem, 1)

    def settle(self):
        self.eng.wait_ge(self.sem, self.base + self.k)


def attention_block(nc, ctx, io, X, CTXH, ID, later_loads, loaded):
    (x, Wq, bq, Wk, bk, Wv, bv, rel, ident_d, flip_d, sel_d, rows_d) = io

    def dram(name, shape):
        return nc.dram_tensor(name, shape, F32, kind="Internal").ap()

    QD, KD = dram("q_parts", (2, B * D, S)), dram("k_parts", (2, B * D, S))
    LD = dram("step_values", (2 * H, 16, S))
    WD = dram("bias_vectors", (2 * H, 3, WCOLS))
    MD = dram("row_maxima", (PAIRS, 2, 2, S))

    def sb(name, shape, dt=F32):
        return ctx.enter_context(nc.sbuf_tensor("sb_" + name, shape, dt))

    def pb(name, shape):
        return ctx.enter_context(nc.psum_tensor(name, shape, F32))

    def sem(name):
        return ctx.enter_context(nc.semaphore(name))

    XT = sb("xn_T", [128, B * S])
    WQ, WK, WV = sb("wq", [D, D]), sb("wk", [D, D]), sb("wv", [D, D])
    BQ, BQS, BK, BV = sb("bq_col", [D, 1]), sb("bq_scaled", [D, 1]), sb("bk_col", [D, 1]), sb("bv_rows", [128, D])
    REL, SEL = sb("rel", [NB, 2 * H]), sb("sel", [NB, WCOLS])
    FLIP, FLIPR = sb("flip", [128, 128]), sb("flip_r", [128, 128], F32R)
    ROWS = sb("rows", [48, S])
    W3 = sb("bias_w", [2 * H, 3, WCOLS])
    VH = sb("v_by_pair", [128, PAIRS, NBLK, 16])
    QP, KP = sb("q_hi_lo", [128, 2, 2, 512]), sb("k_hi_lo", [128, 2, 2, 512])
    ST, MV = sb("ln_stats", [128, 16, 6]), sb("ln_mv", [128, 16, 2])
    VE, RSTD, MHALF = sb("ln_ve", [128, 16]), sb("ln_rstd", [128, 16]), sb("minus_half", [128, 16])
    QO, KO = sb("q_operand", [128, 3, 2, S], F32R), sb("k_operand", [128, 3, 2, S], F32R)
    TT = sb("bias_tables", [128, 3, 2, 3, 160], F32R)
    VB = sb("v_operand", [128, 3, 2, NBLK, 32])
    P = sb("probs", [128, 2, 2, S])
    XN, ZERO = P[:, 0, :, :].rearrange("p a (n d) -> p (a n) d", d=D), P[:, 1, 0, :]
    QF, KF = P[:, 1, 1, 0:512], P[:, 1, 1, 512:S]
    SC = sb("band_scores", [128, 2, 160])
    MX = sb("max_parts", [128, 3, 2, NBLK, 5])
    M, MHL, MR = sb("row_max", [128, 2, NBLK]), sb("max_hi_lo", [128, 2, 2, NBLK]), sb("max_rows", [32, 128])
    CT, RC = sb("context_T", [128, 512]), sb("inv_sum", [128, 4, 4])

    PA = [pb(f"psA{n}", [128, 512]) for n in range(3)]
    PB = [pb(f"psB{n}", [128, 512]) for n in range(3)]
    PV, PM = pb("psV", [128, 512]), pb("psM", [128, 512])

    names = ("w_in bias_in zero_ready half_ready x_ve x_rstd xn_ready xt_psum xt_ready q_psum k_psum v_psum qk_read v_read "
             "qk_split w_psum w_ready w_out step_out rows_ready flip_ready vb_zero vb_ready a_ready a_used "
             "b_ready exp_done pv_done evac_done max_parts max_psum max_rows max_out max_in ctx_psum ctx_used "
             "zeroed bq_scaled m_step r_step own_v").split()
    s = {n: sem(n) for n in names}
    x_in = [sem(f"x_in{n}") for n in range(4)]
    qk_out = [sem(f"qk_out{n}") for n in range(2)]
    ops_in = [sem(f"ops_in{n}") for n in range(3)]
    LOADS = 11
    AHEAD = 5

    Q_BANKS, K_BANKS, V_BANKS = PB[0:2], PA[1:3], (PV, PB[2])

    def bank(ring, p, n):
        return ring[(32 * p.r + n) % 3]

    x_v = x.rearrange("b (n p) d -> p (b n) d", p=128)
    LD_rows = LD.rearrange("h r t -> (h r t)").rearrange("(c p z) -> c p z", c=4, p=128)
    qd = QD.rearrange("a (n h d) t -> a d n h t", h=2, d=DH)
    kd = KD.rearrange("a (n h d) t -> a d n h t", h=2, d=DH)
    ld = LD.rearrange("(n h) r t -> r n h t", h=2)

    def steady(eng, do_pair):
        do_pair(Pair(0, 0), first=True)
        with eng.Fori(0, 4) as i:
            for r in range(1, 4):
                do_pair(Pair(i, r))
        do_pair(Pair(0, 13))
        do_pair(Pair(0, 14), left=1)
        do_pair(Pair(0, 15), left=0)

    block = ctx.enter_context(nc.Block())

    @block.sync
    def _(sp):
        for c in range(4):
            sp.dma_start(X[:, 4 * c:4 * c + 4, :], x_v[:, 4 * c:4 * c + 4, :]).then_inc(x_in[c], 16)
        for w, d in ((ID, ident_d), (WQ, Wq), (WK, Wk), (WV, Wv), (BQ, bq.rearrange("(p o) -> p o", o=1)),
                     (BK, bk.rearrange("(p o) -> p o", o=1)), (BV, bv.partition_broadcast(128))):
            sp.dma_start(w[:, :], d).then_inc(s["w_in"], 16)
        for w, d in ((SEL, sel_d), (REL[:, 0:H], rel), (REL[:, H:2 * H], rel), (FLIP, flip_d), (ROWS[32:48, :], rows_d)):
            sp.dma_start(w[:, :], d).then_inc(s["bias_in"], 16)
        sp.wait_ge(s["zero_ready"], 1)
        for c in range(4):
            sp.dma_start(LD_rows[c], ZERO).then_inc(s["step_out"], 16)

        def parts_out(c):
            b, half = c // 2, c % 2
            sp.wait_ge(s["qk_split"], 4 * (c + 1))
            for dst, src in ((QD, QP), (KD, KP)):
                for part in range(2):
                    sp.dma_start(dst[part, b * D:b * D + D, half * 512:half * 512 + 512],
                                 src[:, c % 2, part, :]).then_inc(qk_out[c % 2], 16)

        parts_out(0)
        sp.wait_ge(s["w_ready"], 3)
        sp.dma_start(WD[:], W3[:]).then_inc(s["w_out"], 16)
        sp.wait_ge(s["step_out"], 64)
        for r in range(1, NBLK):
            sp.dma_start(LD[:, 2 * (r - 1):2 * r, 128 * r:128 * r + 128],
                         W3[:, 1:3, STEP:STEP + 128]).then_inc(s["step_out"], 16)
        parts_out(1)

        def load(p):
            q, k = QO[:, p.set, :, :].bitcast(F32), KO[:, p.set, :, :].bitcast(F32)
            one = bass.ds(p.n, 1)
            for n, (qpart, kpart) in enumerate(((0, 0), (0, 1), (1, 0), (1, 1))):
                rows = slice(DH * n, DH * n + DH)
                sp.dma_start(q[rows], qd[qpart][:, one].rearrange("d o h t -> d (o h) t")).then_inc(ops_in[p.set], 16)
                sp.dma_start(k[rows], kd[kpart][:, one].rearrange("d o h t -> d (o h) t")).then_inc(ops_in[p.set], 16)
            sp.dma_start(q[ROW_STEP:ROW_STEP + 16], ld[:, one].rearrange("r o h t -> r (o h) t")
                         ).then_inc(ops_in[p.set], 16)
            t = TT[:, p.set, :, :, :].bitcast(F32).rearrange("p h a c -> p (h a) c")
            for at, seg, n in ((0, DIAG, 128), (128, EDGE, 32)):
                sp.dma_start(t[:, :, at:at + n], bass.AP(WD.tensor, p.n * (2 * 3 * WCOLS) + seg,
                                                         [[1, 128], [WCOLS, 6], [1, n]])).then_inc(ops_in[p.set], 16)

        def maxima(p):
            sp.wait_ge(s["max_rows"], p.n + 1)
            sp.dma_start(MD.rearrange("n a h (t q) -> n (a h t) q", q=128)[bass.ds(p.n, 1)]
                         .rearrange("o r q -> (o r) q"), MR[:]).then_inc(s["max_out"], 16)
            sp.wait_ge(s["max_out"], p.n * 16 + 16)
            sp.dma_start(QO[ROW_MAX:ROW_MAX + 2, p.set, :, :].bitcast(F32),
                         MD.rearrange("n a h t -> a n h t")[:, bass.ds(p.n, 1)].rearrange("a o h t -> a (o h) t")
                         ).then_inc(s["max_in"], 16)

        for out in qk_out:
            sp.wait_ge(out, 16 * 4)
        sp.wait_ge(s["w_out"], 16)
        sp.wait_ge(s["step_out"], 16 * (4 + 7))
        sp.wait_ge(s["rows_ready"], 3)
        sp.wait_ge(s["zeroed"], 2)
        load(Pair(0, 0))
        load(Pair(0, 1))
        parts_out(2)
        parts_out(3)
        for out in qk_out:
            sp.wait_ge(out, 16 * 8)
        maxima(Pair(0, 0))
        for dst, src in later_loads:
            sp.dma_start(dst, src).then_inc(loaded, 16)

        def do_pair(p, first=False, left=2):
            if left == 2:
                if not first:
                    sp.wait_ge(s["b_ready"], p.n * 32)
                load(p + 2)
            if left:
                maxima(p + 1)

        steady(sp, do_pair)

    @block.gpsimd
    def _(pool):
        pool.memset(MHALF[:], -0.5).then_inc(s["half_ready"], 1)
        pool.memset(ZERO, 0.0).then_inc(s["zero_ready"], 1)
        pool.wait_ge(s["half_ready"], 1)
        pool.wait_ge(s["x_ve"], 1)
        pool.tensor_tensor(RSTD[:], VE[:], MHALF[:], ALU.pow).then_inc(s["x_rstd"], 1)
        pool.memset(KO[:].bitcast(U32), 0).then_inc(s["zeroed"], 1)
        pool.memset(QO[:].bitcast(U32), 0).then_inc(s["zeroed"], 1)
        pool.memset(VB[:], 0.0).then_inc(s["vb_zero"], 1)
        pool.wait_ge(s["vb_zero"], 1)
        pool.memset(VB[:, :, :, :, DH:DH + 1], 1.0).then_inc(s["vb_zero"], 1)
        pool.wait_ge(s["v_read"], 4)
        pool.wait_ge(s["vb_zero"], 2)

        def values(p):
            for a in range(2):
                pool.tensor_copy(VB[:, p.set, a, :, 0:DH],
                                 VH[:, bass.ds(p.n, 1), :, a * DH:a * DH + DH].rearrange("p o n c -> p (o n) c")
                                 ).then_inc(s["vb_ready"], 1)

        values(Pair(0, 0))

        def do_pair(p, first=False, left=2):
            if left:
                if not first:
                    pool.wait_ge(s["pv_done"], (p.n - 1) * NBLK + 1)
                values(p + 1)

        steady(pool, do_pair)

    @block.scalar
    def _(act):
        act.wait_ge(s["w_in"], 16 * 7)
        nc.scalar.activation(BQS[:], BQ[:], ACT.Identity, scale=DH ** -0.5).then_inc(s["bq_scaled"], 1)
        for c in range(4):
            act.wait_ge(s["xt_psum"], c + 1)
            nc.scalar.copy(XT[:, 512 * c:512 * c + 512], PM[:]).then_inc(s["xt_ready"], 1)
            if c == 0:
                act.wait_ge(s["w_psum"], 1)
                nc.scalar.copy(W3[:, 0, 0:512], PA[0][0:2 * H, :])
                nc.scalar.copy(W3[:, 0, 512:WCOLS], PB[2][0:2 * H, 0:WCOLS - 512]).then_inc(s["w_ready"], 1)
            if c:
                act.wait_ge(s["qk_split"], 4 * c)
            act.wait_ge(s["q_psum"], c + 1)
            act.wait_ge(s["bq_scaled"], 1)
            nc.scalar.activation(QF, Q_BANKS[c % 2][:], ACT.Identity, bias=BQS[:, 0:1], scale=DH ** -0.5
                                 ).then_inc(s["qk_read"], 1)
            act.wait_ge(s["k_psum"], c + 1)
            nc.scalar.activation(KF, K_BANKS[c % 2][:], ACT.Identity, bias=BK[:, 0:1]).then_inc(s["qk_read"], 1)

        def max_copy(p):
            act.wait_ge(s["max_psum"], p.n + 1)
            act.wait_ge(s["max_out"], p.n * 16)
            nc.scalar.copy(MR[:], PM[0:32, 0:128]).then_inc(s["max_rows"], 1)

        def evacuate(p):
            act.wait_ge(s["pv_done"], p.n * NBLK + NBLK)
            nc.scalar.copy(CT[:], PV[:]).then_inc(s["evac_done"], 1)

        max_copy(Pair(0, 0))

        def do_pair(p, first=False, left=2):
            for j in range(2 * NBLK):
                kb, a = j // 2, j % 2
                for half in range(2):
                    act.wait_ge(s["b_ready"], p.n * 32 + (2 * j + half + 1))
                    if half == 0 and a == 0 and not (first and kb < 2):
                        act.wait_ge(s["pv_done"], p.n * NBLK + (kb - 1))
                    nc.scalar.activation(P[:, kb % 2, a, half * 512:half * 512 + 512], bank(PB, p, 2 * j + half)[:],
                                         ACT.Exp).then_inc(s["exp_done"], 1)
                if j == 1 and not first:
                    evacuate(p + -1)
                if j == 2 * NBLK - AHEAD + 1 and left:
                    max_copy(p + 1)

        steady(act, do_pair)
        evacuate(Pair(0, 15))

    @block.tensor
    def _(pe):
        for c in range(4):
            pe.wait_ge(s["xn_ready"], 4 * c + 4)
            if c == 0:
                pe.wait_ge(s["w_in"], 16 * 7)
            else:
                pe.wait_ge(s["xt_ready"], c)
            for n in range(4):
                ins = nc.tensor.transpose(PM[:, 128 * n:128 * n + 128], XN[:, 4 * c + n, :], ID[:])
            ins.then_inc(s["xt_psum"], 1)
            pe.wait_ge(s["xt_ready"], c + 1)
            if c >= 2:
                pe.wait_ge(s["qk_read"], 2 * (c - 1))
                pe.wait_ge(s["v_read"], c - 1)
            xt = XT[:, 512 * c:512 * c + 512]
            nc.tensor.matmul(Q_BANKS[c % 2][:], WQ[:], xt, start=True, stop=True).then_inc(s["q_psum"], 1)
            nc.tensor.matmul(K_BANKS[c % 2][:], WK[:], xt, start=True, stop=True).then_inc(s["k_psum"], 1)
            if c == 1:
                pe.wait_ge(s["w_ready"], 1)
            for n in range(4):
                ins = nc.tensor.matmul(V_BANKS[c % 2][:, 128 * n:128 * n + 128], xt[:, 128 * n:128 * n + 128], WV[:],
                                       start=True, stop=True)
            ins.then_inc(s["v_psum"], 1)
            if c == 0:
                pe.wait_ge(s["bias_in"], 16 * 5)
                for at, out in ((0, PA[0]), (512, PB[2])):
                    end = min(at + 512, WCOLS)
                    ins = nc.tensor.matmul(out[0:2 * H, 0:end - at], REL[:], SEL[:, at:end], start=True, stop=True)
                ins.then_inc(s["w_psum"], 1)

        def scores(p, t, half):
            a, qb = t // NBLK, t % NBLK
            if t == 0 and half == 0:
                pe.wait_ge(ops_in[p.set], p.use * (16 * LOADS) + 16 * LOADS)
            n = 2 * t + half
            if n > 2 or p.r > 0:
                pe.wait_ge(s["a_used"], p.n * 32 + (n - 2))
            nc.tensor.matmul(bank(PA, p, n)[:], QO[:, p.set, a, 128 * qb:128 * qb + 128],
                             KO[:, p.set, a, half * 512:half * 512 + 512], start=True, stop=True
                             ).then_inc(s["a_ready"], 1)

        def scores_T(p, j, half, first):
            kb, a = j // 2, j % 2
            n = 2 * j + half
            if not (first and n < 3):
                pe.wait_ge(s["exp_done"], p.n * 32 + (n - 2))
            out = bank(PB, p, n)
            lo, hi = half * 512, half * 512 + 512
            c0, c1 = max(lo, 128 * kb), min(hi, 128 * kb + 160)
            ins = nc.tensor.matmul(out[:], KO[:, p.set, a, 128 * kb:128 * kb + 128], QO[:, p.set, a, lo:hi],
                                   start=True, stop=c0 >= c1)
            if c0 < c1:
                for part in (1, 2):
                    ins = nc.tensor.matmul(out[:, c0 - lo:c1 - lo], FLIPR[:],
                                           TT[:, p.set, a, part, c0 - 128 * kb:c1 - 128 * kb],
                                           start=False, stop=part == 2)
            ins.then_inc(s["b_ready"], 1)

        def values(p, kb):
            pe.wait_ge(s["exp_done"], p.n * 32 + (4 * kb + 4))
            if kb == 0:
                pe.wait_ge(s["vb_ready"], p.n * 2 + 2)
                if p.r:
                    pe.wait_ge(s["evac_done"], p.n)
            for a in range(2):
                for half in range(2):
                    g = 32 * (2 * a + half)
                    ins = nc.tensor.matmul(PV[g:g + 32, :], VB[:, p.set, a, kb, :],
                                           P[:, kb % 2, a, half * 512:half * 512 + 512],
                                           start=kb == 0, stop=kb == NBLK - 1, tile_position=(0, g))
            ins.then_inc(s["pv_done"], 1)

        def max_transpose(p):
            pe.wait_ge(s["max_parts"], p.n + 1)
            if p.r > 1:
                pe.wait_ge(s["ctx_used"], p.n - 1)
            nc.tensor.transpose(PM[0:32, 0:128], MHL[:].rearrange("p a h t -> p (a h t)"), ID[:]
                                ).then_inc(s["max_psum"], 1)

        def context_transpose(p):
            pe.wait_ge(s["evac_done"], p.n + 1)
            if p.r < PAIRS - 1:
                pe.wait_ge(s["max_rows"], p.n + 2)
            else:
                pe.wait_ge(s["ctx_used"], p.n)
            for c in range(4):
                ins = nc.tensor.transpose(PM[:, 128 * c:128 * c + 128], CT[:, 128 * c:128 * c + 128], ID[:])
            ins.then_inc(s["ctx_psum"], 1)

        pe.wait_ge(s["rows_ready"], 3)
        pe.wait_ge(s["flip_ready"], 1)
        pe.wait_ge(s["qk_read"], 8)
        pe.wait_ge(s["v_read"], 4)
        pe.wait_ge(s["w_ready"], 3)
        for t in range(16 + AHEAD):
            for half in range(2):
                scores(Pair(0, t // 16), t % 16, half)
        max_transpose(Pair(0, 0))

        def do_pair(p, first=False, left=2):
            for j in range(2 * NBLK):
                t = j + AHEAD
                if j == 0:
                    pe.wait_ge(s["max_in"], p.n * 16 + 16)
                for half in range(2):
                    scores_T(p, j, half, first)
                    if t < 16 and left:
                        scores(p + 1, t, half)
                    if t >= 16 and left == 2:
                        scores(p + 2, t - 16, half)
                if j == 0 and not first:
                    values(p + -1, NBLK - 1)
                if j % 2 == 0 and j:
                    values(p, j // 2 - 1)
                if j == 3 and not first:
                    context_transpose(p + -1)
                if j == 2 * NBLK - AHEAD + 1 and left:
                    max_transpose(p + 1)

        steady(pe, do_pair)
        values(Pair(0, 15), NBLK - 1)
        context_transpose(Pair(0, 15))

    @block.vector
    def _(dve):
        own = Chain(dve, s["own_v"])
        own.mark(nc.vector.memset(MX[:], -3.0e38))
        for c in range(4):
            dve.wait_ge(x_in[c], 16)
            for n in range(4 * c, 4 * c + 4):
                own.mark(nc.vector.bn_stats(ST[:, n, :], X[:, n, :]))
        own.settle()
        for n in range(16):
            own.mark(nc.vector.bn_aggr(MV[:, n, :], ST[:, n, :]))
        own.settle()
        nc.vector.tensor_scalar(VE[:], MV[:, :, 1], EPS, None, ALU.add).then_inc(s["x_ve"], 1)
        dve.wait_ge(s["x_rstd"], 1)
        for n in range(16):
            nc.vector.tensor_scalar(XN[:, n, :], X[:, n, :], MV[:, n, 0:1], RSTD[:, n:n + 1],
                                    ALU.subtract, ALU.mult).then_inc(s["xn_ready"], 1)
        dve.wait_ge(s["bias_in"], 16 * 5)
        nc.vector.tensor_copy(FLIPR[:], FLIP[:]).then_inc(s["flip_ready"], 1)
        dve.wait_ge(s["zeroed"], 1)
        for m in range(3):
            nc.vector.tensor_copy(KO[32:48, m, :, :], ROWS[32:48, :].rearrange("r (o t) -> r o t", o=1)
                                  .to_broadcast([16, 2, S])).then_inc(s["rows_ready"], 1)
        dve.wait_ge(s["w_in"], 16 * 7)
        for c in range(4):
            if c >= 2:
                dve.wait_ge(qk_out[c % 2], 64 * (c // 2))
            dve.wait_ge(s["qk_read"], 2 * c + 2)
            for full, parts in ((QF, QP), (KF, KP)):
                nc.vector.tensor_copy(parts[:, c % 2, 0, :].bitcast(F32R), full[:]).then_inc(s["qk_split"], 1)
            dve.wait_ge(s["qk_split"], 4 * c + 2)
            for full, parts in ((QF, QP), (KF, KP)):
                nc.vector.tensor_tensor(parts[:, c % 2, 1, :].bitcast(F32R), full[:], parts[:, c % 2, 0, :],
                                        ALU.subtract).then_inc(s["qk_split"], 1)
            dve.wait_ge(s["v_psum"], c + 1)
            for n in range(4):
                blk = 4 * (c % 2) + n
                ins = nc.vector.tensor_tensor(
                    VH[:, 8 * (c // 2):8 * (c // 2) + 8, blk, :],
                    V_BANKS[c % 2][:, 128 * n:128 * n + 128].rearrange("p (m c) -> p m c", c=16),
                    BV[:].rearrange("p (m c) -> p m c", c=16), ALU.add)
            ins.then_inc(s["v_read"], 1)
            if c == 0:
                dve.wait_ge(s["w_ready"], 1)
                nc.vector.tensor_copy(W3[:, 1, :].bitcast(F32R), W3[:, 0, :]).then_inc(s["w_ready"], 1)
                dve.wait_ge(s["w_ready"], 2)
                nc.vector.tensor_tensor(W3[:, 2, :].bitcast(F32R), W3[:, 0, :], W3[:, 1, :], ALU.subtract
                                        ).then_inc(s["w_ready"], 1)

        def reversed_table(p, a, c0, c1):
            view = TT[:, p.set, a, 0, 159 - c0:160 - c0].bitcast(F32)
            return bass.AP(view.tensor, view.offset, [list(view.ap[0]), [-1, c1 - c0]])

        def tile_max(p, t):
            a, qb = t // NBLK, t % NBLK
            left, right = 128 * qb - BAND, 128 * qb + 128
            mx = MX[:, p.set, a, qb, :]
            for half in range(2):
                n, lo, hi = 2 * t + half, half * 512, half * 512 + 512
                ps = bank(PA, p, n)
                before, after = (lo, min(hi, left), half), (max(lo, right), hi, 2 + half)
                c0, c1 = max(lo, left), min(hi, right)
                if c0 < c1 and (t > 1 or p.r):
                    dve.wait_ge(s["a_used"], p.n * 32 + 2 * (t - 1))
                dve.wait_ge(s["a_ready"], p.n * 32 + (n + 1))
                for begin, end, slot in (before, after):
                    if begin < end:
                        ins = nc.vector.tensor_reduce(mx[:, slot:slot + 1], ps[:, begin - lo:end - lo], AX.X, ALU.max)
                if c0 < c1:
                    slot = 1 if qb == NBLK // 2 and half else 4
                    ins = nc.vector.tensor_tensor_reduce(
                        SC[:, t % 2, c0 - left:c1 - left], ps[:, c0 - lo:c1 - lo],
                        reversed_table(p, a, c0 - left, c1 - left), 1.0, -3.0e38, ALU.add, ALU.max,
                        mx[:, slot:slot + 1])
                ins.then_inc(s["a_used"], 1)

        def pair_max(p):
            dve.wait_ge(s["a_used"], p.n * 32 + 32)
            nc.vector.tensor_reduce(M[:], MX[:, p.set, :, :, :], AX.X, ALU.max).then_inc(s["m_step"], 1)
            if p.r:
                dve.wait_ge(s["max_psum"], p.n)
            dve.wait_ge(s["m_step"], p.n * 2 + 1)
            nc.vector.tensor_scalar(MHL[:, 0, :, :].bitcast(F32R), M[:], -1.0, None, ALU.mult
                                    ).then_inc(s["m_step"], 1)
            dve.wait_ge(s["m_step"], p.n * 2 + 2)
            nc.vector.scalar_tensor_tensor(MHL[:, 1, :, :].bitcast(F32R), M[:], -1.0, MHL[:, 0, :, :],
                                           ALU.mult, ALU.subtract).then_inc(s["max_parts"], 1)

        def context(p):
            view = PM[:].rearrange("p (c a h w) -> p a h c w", c=4, a=2, h=2)
            dve.wait_ge(s["ctx_psum"], p.n + 1)
            nc.vector.reciprocal(RC[:].rearrange("p c g -> p g c"),
                                 PM[:].rearrange("p (c g w) -> p g c w", c=4, g=4)[:, :, :, DH]
                                 ).then_inc(s["r_step"], 1)
            dve.wait_ge(s["r_step"], p.n + 1)
            for a in range(2):
                out = CTXH[:, bass.ds(p.n, 1), :, a * DH:a * DH + DH].rearrange("p o (h c) w -> p (o h) c w", h=2)
                inv = RC[:].rearrange("p c (a h o) -> p a h c o", a=2, o=1)[:, a].to_broadcast([128, 2, 4, DH])
                ins = nc.vector.tensor_tensor(out, view[:, a, :, :, 0:DH], inv, ALU.mult)
            ins.then_inc(s["ctx_used"], 1)

        own.settle()
        for t in range(16):
            if t == 0:
                dve.wait_ge(ops_in[0], 16 * LOADS)
            tile_max(Pair(0, 0), t)
        pair_max(Pair(0, 0))
        for t in range(AHEAD):
            if t == 0:
                dve.wait_ge(ops_in[1], 16 * LOADS)
            tile_max(Pair(0, 1), t)

        def do_pair(p, first=False, left=2):
            for j in range(2 * NBLK):
                t = j + AHEAD
                if t < 16 and left:
                    tile_max(p + 1, t)
                    if t == 15:
                        pair_max(p + 1)
                if t >= 16 and left == 2:
                    if t == 16:
                        q = p + 2
                        dve.wait_ge(ops_in[q.set], q.use * (16 * LOADS) + 16 * LOADS)
                    tile_max(p + 2, t - 16)
                if j == 4 and not first:
                    context(p + -1)

        steady(dve, do_pair)
        context(Pair(0, 15))


FF = 512
NE, HID = 8, 352
MROWS = (128, 128, 96)
CH = 4
PARTS = 3 * NE
AT = {"norm1": 2, "transpose1": 3, "mix_prev": 4, "mix_now": 5, "k_r": 6, "square": 6, "v": 7, "channel_out": 8,
      "stats2": 8, "norm2": 9, "norm3": 11, "spiral1": 11, "spiral2": 14, "stats4": 14, "norm4": 17,
      "transpose2": 18, "hidden1": 19, "hidden2": 20, "mlp_out": 21, "x3": 21, "norm5": 22, "transpose3": 23}


def tail_weights(nc, ctx, w):
    def sb(name, shape):
        return ctx.enter_context(nc.sbuf_tensor("wt_" + name, shape, F32))

    t = {"r": sb("r", [D, D]), "k": sb("k", [D, D]), "v": sb("v", [D, D]),
         "mu": sb("mu", [D, 2]), "rows": sb("rows", [128, 6, D]), "l1": sb("l1", [D, FF]), "b1": sb("b1", [128, 4]),
         "l2": sb("l2", [128, 4, D]), "gate": sb("gate", [D, NE]), "iota": sb("iota", [128, NE]),
         "w1": sb("w1", [D, NE, HID]), "w3": sb("w3", [D, NE, HID]), "w2": sb("w2", [128, NE, 3, D])}
    loads = [(t["r"][:], w["W_r"]), (t["k"][:], w["W_k"]), (t["v"][:], w["W_v"]),
             (t["mu"][:, 0:1], w["mu_r"].rearrange("(p o) -> p o", o=1)),
             (t["mu"][:, 1:2], w["mu_k"].rearrange("(p o) -> p o", o=1)),
             (t["l1"][:], w["l1_w1"]), (t["b1"][:], w["b1"]),
             (t["l2"][:], w["l1_w2"].rearrange("(m p) d -> p m d", p=128)),
             (t["gate"][:], w["gate_w"]), (t["iota"][:], w["iota"].partition_broadcast(128)),
             (t["w1"][:], w["w1"]), (t["w3"][:], w["w3"])]
    for n, name in enumerate(("lmlg", "theta", "init", "ln_w", "ln_b", "b2")):
        loads.append((t["rows"][:, n, :], w[name].partition_broadcast(128)))
    for m, rows in enumerate(MROWS):
        loads.append((t["w2"][0:rows, :, m, :], w["w2"][:, 128 * m:128 * m + rows, :].rearrange("e p d -> p e d")))
    return t, loads


def tail_block(nc, ctx, t, n_loads, loaded, ident, X, CTXH, out):
    def sb(name, shape, dt=F32):
        return ctx.enter_context(nc.sbuf_tensor("t_" + name, shape, dt))

    def pb(name):
        return ctx.enter_context(nc.psum_tensor(name, [128, 512], F32))

    names = ("w_high w_low xm_parts own_c own_p own_r own_g gamma angle cosine gap gap_exp ve rstd xn1 t1 xnt "
             "mixed r_psum k_psum sig relu ka v_psum y_done acc_done h2 t2 h2t up_hid hid l2_psum x3 xm t3 "
             "xmt logits up_u up_v silu hm down added stored half").split()
    s = {n: ctx.enter_context(nc.semaphore("t_" + n)) for n in names}

    X1, X2, X3, XN = sb("x1", [128, 4, D]), sb("x2", [128, 4, D]), sb("x3", [128, 4, D]), sb("xn", [128, 4, D])
    ST, MV, VE, RSTD = sb("st", [128, 4, 6]), sb("mv", [128, 4, 2]), sb("ve", [128, 4]), sb("rstd", [128, 4])
    MHALF, HOLD = sb("mhalf", [128, 4]), sb("hold", [128, 3])
    XNT = sb("xnt", [128, 2, 257])
    MU1 = sb("mu1", [128, 2])
    XR, XK = sb("xr", [128, 2, 256]), sb("xk", [128, 2, 256])
    KR, KA, RS = sb("kr", [128, 512]), sb("ka", [128, 512]), sb("rs", [128, 4, D])
    A, HH, U, Y, ACC = (sb(n, [128, 4, D]) for n in ("a", "h", "u", "y", "acc"))
    H2T, HIDT, XMT = sb("h2t", [128, 512]), sb("hidt", [128, 4, 512]), sb("xmt", [128, 512])
    XMH, XML = sb("xm_high", [128, 512], F32R), sb("xm_low", [128, 512], F32R)
    HIGH = {n: sb(n + "_high", [D, NE, HID], F32R) for n in ("w1", "w3")}
    LOW = {n: sb(n + "_low", [D, NE, HID], F32R) for n in ("w1", "w3")}
    CR, CI, CI2 = sb("cr", [128, D]), sb("ci", [128, D]), sb("ci2", [128, D])
    W1, W2, W4, W5 = (sb(f"work{n}", [128, D]) for n in range(4))
    LG, M8, I8, IF = sb("lg", [128, 4, 8]), sb("m8", [128, 4, 8]), sb("i8", [128, 4, 8], U32), sb("if", [128, 4, 2])
    DL, EX, SM, RW, EW = (sb(n, [128, 4]) for n in ("dl", "ex", "sm", "rw", "ew"))
    E1, E2, G = sb("e1", [128, 4, NE]), sb("e2", [128, 4, NE]), sb("g", [128, 4, NE])
    SU, HM = sb("su", [128, 2, 512]), sb("hm", [128, 2, 3, 512])
    OUT = sb("out", [128, 4, D])
    PU, PVV, PY = [pb("pu0"), pb("pu1")], [pb("pv0"), pb("pv1")], [pb("py0"), pb("py1")]
    R0, R1 = pb("pr0"), pb("pr1")
    LMLG, THETA, INIT, LNW, LNB, B2 = (t["rows"][:, n, :] for n in range(6))

    def wide(row):
        return row.rearrange("p (o d) -> p o d", o=1).to_broadcast([128, 4, D])

    def wide2(row):
        return row.rearrange("p (o d) -> p o d", o=1).to_broadcast([128, 2, D])

    NORMS = 5
    out_v = out.rearrange("b (n p) d -> p b n d", p=128)
    block = ctx.enter_context(nc.Block())

    def run(eng, before, part, after):
        for k in range(PARTS):
            part(-1, k, False, True)
        before(0)
        with eng.Fori(0, CH - 1) as c:
            for k in range(PARTS):
                part(c, k, True, True)
            after(c)
            before(c + 1)
        for k in range(PARTS):
            part(CH - 1, k, True, False)
        after(CH - 1)

    @block.sync
    def _(sp):
        with sp.Fori(0, CH) as c:
            sp.wait_ge(s["added"], c * NE + (NE + 2))
            for b in range(B):
                sp.dma_start(out_v[:, b, bass.ds(2 * c, 2), :], OUT[:, 2 * b:2 * b + 2, :]).then_inc(s["stored"], 16)
        sp.wait_ge(s["stored"], CH * 32 + 16)

    @block.gpsimd
    def _(pool):
        pool.memset(MHALF[:], -0.5).then_inc(s["half"], 1)
        pool.wait_ge(s["half"], 1)

        def rstd(c, n):
            pool.wait_ge(s["ve"], c * NORMS + (n + 1))
            pool.tensor_tensor(RSTD[:], VE[:], MHALF[:], ALU.pow).then_inc(s["rstd"], 1)

        def chunk(c, first=False):
            for n in range(4):
                rstd(c, n)
                if first and n == 0:
                    for m, w in enumerate(("w1", "w3")):
                        pool.wait_ge(s["w_high"], m + 1)
                        pool.tensor_tensor(LOW[w][:], t[w][:], HIGH[w][:].bitcast(F32), ALU.subtract
                                           ).then_inc(s["w_low"], 1)
            pool.wait_ge(s["y_done"], c + 1)
            pool.tensor_tensor(ACC[:], X2[:], Y[:], ALU.add).then_inc(s["own_p"], 1)
            pool.wait_ge(s["own_p"], c + 1)
            pool.tensor_tensor(ACC[:], ACC[:], wide(B2), ALU.add).then_inc(s["acc_done"], 1)
            rstd(c, 4)

        chunk(0, first=True)
        with pool.Fori(1, CH) as c:
            chunk(c)

    @block.scalar
    def _(act):
        act.wait_ge(loaded, 16 * n_loads)
        nc.scalar.activation(W1[:], LMLG, ACT.Exp).then_inc(s["gamma"], 1)
        act.wait_ge(s["gamma"], 1)
        nc.scalar.activation(W2[:], W1[:], ACT.Exp, scale=-1.0).then_inc(s["gamma"], 1)
        act.wait_ge(s["angle"], 1)
        nc.scalar.activation(W5[:], W4[:], ACT.Sin, scale=float(2 * np.pi)).then_inc(s["cosine"], 1)
        for w in ("w1", "w3"):
            nc.scalar.copy(HIGH[w][:], t[w][:]).then_inc(s["w_high"], 1)

        def part(c, k, moe, pre):
            if moe:
                n = c * PARTS + (k + 1)
                rows = MROWS[k % 3]
                act.wait_ge(s["up_u"], n)
                act.wait_ge(s["hm"], n)
                nc.scalar.activation(SU[0:rows, k % 2, :], PU[k % 2][0:rows, :], ACT.Silu).then_inc(s["silu"], 1)
            if pre:
                d = c + 1
                if k == AT["transpose1"]:
                    act.wait_ge(s["t1"], d + 1)
                    act.wait_ge(s["mixed"], d)
                    nc.scalar.copy(XNT[:, :, 1:257], R0[:].rearrange("p (b t) -> p b t", b=2)).then_inc(s["xnt"], 1)
                if k == AT["k_r"]:
                    act.wait_ge(s["k_psum"], d + 1)
                    nc.scalar.activation(KR[:], R0[:], ACT.Relu).then_inc(s["relu"], 1)
                    act.wait_ge(s["r_psum"], d + 1)
                    nc.scalar.activation(RS[:].rearrange("p g d -> p (g d)"), R1[:], ACT.Sigmoid).then_inc(s["sig"], 1)
                if k == AT["transpose2"]:
                    act.wait_ge(s["t2"], d + 1)
                    nc.scalar.copy(H2T[:], R1[:]).then_inc(s["h2t"], 1)
                if k in (AT["hidden1"], AT["hidden2"]):
                    for m in (0, 1) if k == AT["hidden1"] else (2, 3):
                        act.wait_ge(s["up_hid"], d * 4 + (m + 1))
                        if m == 0:
                            act.wait_ge(s["l2_psum"], d)
                        nc.scalar.activation(HIDT[:, m, :], (R0, R1)[m % 2][:], ACT.Silu, bias=t["b1"][:, m:m + 1]
                                             ).then_inc(s["hid"], 1)

        def to_experts(c):
            act.wait_ge(s["t3"], c + 1)
            nc.scalar.copy(XMT[:], R1[:]).then_inc(s["xmt"], 1)
            act.wait_ge(s["gap"], c + 1)
            nc.scalar.activation(EX[:], DL[:], ACT.Exp).then_inc(s["gap_exp"], 1)

        act.sem_inc(s["silu"], 2)
        run(act, to_experts, part, lambda c: None)

    @block.tensor
    def _(pe):
        pe.wait_ge(loaded, 16 * n_loads)

        def transpose4(src, dst, done):
            for g in range(4):
                ins = nc.tensor.transpose(dst[:, 128 * g:128 * g + 128], src[:, g, :], ident[:])
            ins.then_inc(done, 1)

        def down(c, e):
            pe.wait_ge(s["hm"], c * PARTS + (3 * e + 3 + 2))
            pe.wait_ge(s["added"], c * NE + (e + 1))
            for g in range(4):
                for m, rows in enumerate(MROWS):
                    ins = nc.tensor.matmul(PY[e % 2][:, 128 * g:128 * g + 128],
                                           HM[0:rows, e % 2, m, 128 * g:128 * g + 128], t["w2"][0:rows, e, m, :],
                                           start=m == 0, stop=m == 2)
            ins.then_inc(s["down"], 1)

        def up(bank, w, e, m):
            rows = MROWS[m]
            high, low = (x[:, e, 128 * m:128 * m + rows] for x in (HIGH[w], LOW[w]))
            for n, (a, b) in enumerate(((high, XMH), (low, XMH), (high, XML))):
                ins = nc.tensor.matmul(bank[0:rows, :], a, b[:], start=n == 0, stop=n == 2)
            return ins

        def part(c, k, moe, pre):
            e, m = k // 3, k % 3
            if moe:
                n = c * PARTS + (k + 1)
                if k == 0:
                    pe.wait_ge(s["xm_parts"], c * 2 + 2)
                pe.wait_ge(s["silu"], n)
                up(PU[k % 2], "w1", e, m).then_inc(s["up_u"], 1)
                pe.wait_ge(s["hm"], n)
                up(PVV[k % 2], "w3", e, m).then_inc(s["up_v"], 1)
                if m == 2 and e:
                    down(c, e - 1)
            if pre:
                d = c + 1
                if k == AT["transpose1"]:
                    pe.wait_ge(s["xn1"], d + 1)
                    transpose4(XN, R0, s["t1"])
                if k == AT["k_r"]:
                    pe.wait_ge(s["mixed"], d + 1)
                    nc.tensor.matmul(R0[:], t["k"][:], XK[:].rearrange("p b t -> p (b t)"), start=True, stop=True
                                     ).then_inc(s["k_psum"], 1)
                    xr = XR[:].rearrange("p b t -> p (b t)")
                    for g in range(4):
                        ins = nc.tensor.matmul(R1[:, 128 * g:128 * g + 128], xr[:, 128 * g:128 * g + 128], t["r"][:],
                                               start=True, stop=True)
                    ins.then_inc(s["r_psum"], 1)
                if k == AT["v"]:
                    pe.wait_ge(s["ka"], d + 1)
                    for g in range(4):
                        ins = nc.tensor.matmul(R0[:, 128 * g:128 * g + 128], KA[:, 128 * g:128 * g + 128], t["v"][:],
                                               start=True, stop=True)
                    ins.then_inc(s["v_psum"], 1)
                if k == AT["transpose2"]:
                    pe.wait_ge(s["sig"], d + 1)
                    pe.wait_ge(s["h2"], d + 1)
                    transpose4(XN, R1, s["t2"])
                if k in (AT["hidden1"], AT["hidden2"]):
                    for m in (0, 1) if k == AT["hidden1"] else (2, 3):
                        if m == 0:
                            pe.wait_ge(s["h2t"], d + 1)
                        if m >= 2:
                            pe.wait_ge(s["hid"], d * 4 + (m - 1))
                        nc.tensor.matmul((R0, R1)[m % 2][:], t["l1"][:, 128 * m:128 * m + 128], H2T[:],
                                         start=True, stop=True).then_inc(s["up_hid"], 1)
                if k == AT["mlp_out"]:
                    pe.wait_ge(s["hid"], d * 4 + 4)
                    for g in range(4):
                        for m in range(4):
                            ins = nc.tensor.matmul(R0[:, 128 * g:128 * g + 128], HIDT[:, m, 128 * g:128 * g + 128],
                                                   t["l2"][:, m, :], start=m == 0, stop=m == 3)
                    ins.then_inc(s["l2_psum"], 1)
                if k == AT["transpose3"]:
                    pe.wait_ge(s["xm"], d + 1)
                    transpose4(XN, R1, s["t3"])

        def after(c):
            down(c, NE - 1)

        def to_experts(c):
            pe.wait_ge(s["w_low"], 2)
            pe.wait_ge(s["xmt"], c + 1)
            for g in range(4):
                ins = nc.tensor.matmul(R0[:, 8 * g:8 * g + 8], XMT[:, 128 * g:128 * g + 128], t["gate"][:],
                                       start=True, stop=True)
            ins.then_inc(s["logits"], 1)

        run(pe, to_experts, part, after)

    @block.vector
    def _(dve):
        V = nc.vector
        dve.sem_inc(s["hm"], 2)
        dve.sem_inc(s["added"], 2)
        dve.sem_inc(s["stored"], 16)
        dve.wait_ge(loaded, 16 * n_loads)
        own = Chain(dve, s["own_c"])
        own.mark(V.tensor_scalar(W4[:], THETA, float(0.5 / np.pi), 0.25, ALU.mult, ALU.add))
        own.mark(V.tensor_scalar(MU1[:], t["mu"][:], -1.0, 1.0, ALU.mult, ALU.add))
        own.mark(V.memset(XNT[:, :, 0:1], 0.0))
        own.settle()
        ROUND = float(1.5 * 2 ** 23)
        own.mark(V.tensor_scalar(W5[:], W4[:], ROUND, ROUND, ALU.add, ALU.subtract))
        own.settle()
        own.mark(V.tensor_tensor(W5[:], W4[:], W5[:], ALU.subtract))
        own.settle()
        V.tensor_scalar(W4[:], W5[:], 0.4999999, -0.4999999, ALU.min, ALU.max).then_inc(s["angle"], 1)

        def spiral_constants():
            dve.wait_ge(s["gamma"], 2)
            dve.wait_ge(s["cosine"], 1)
            own.mark(V.tensor_tensor(CR[:], W2[:], W5[:], ALU.mult))
            own.mark(V.tensor_tensor(W1[:], W2[:], W2[:], ALU.mult))
            own.mark(V.tensor_tensor(W4[:], W5[:], W5[:], ALU.mult))
            own.settle()
            own.mark(V.tensor_tensor(CI[:], CR[:], INIT, ALU.mult))
            own.mark(V.tensor_scalar(W2[:], W4[:], 2.0, -1.0, ALU.mult, ALU.add))
            own.mark(V.tensor_tensor(W5[:], W1[:], INIT, ALU.mult))
            own.settle()
            own.mark(V.tensor_tensor(CI2[:], W5[:], W2[:], ALU.mult))
            own.settle()

        PRE_MARKS, ROUTE_MARKS = 59, 18

        def stats(ch, src):
            for g in range(4):
                ch.mark(V.bn_stats(ST[:, g, :], src[:, g, :]))
            ch.settle()
            V.memset(HOLD[:, 2:3], 0.0)
            for g in range(4):
                ch.mark(V.bn_aggr(MV[:, g, :], ST[:, g, :]))
            ch.settle()
            V.tensor_scalar(VE[:], MV[:, :, 1], EPS, None, ALU.add).then_inc(s["ve"], 1)

        def normed(c, n, src, dst):
            dve.wait_ge(s["rstd"], c * NORMS + (n + 1))
            for g in range(4):
                ins = V.tensor_scalar(dst[:, g, :], src[:, g, :], MV[:, g, 0:1], RSTD[:, g:g + 1],
                                      ALU.subtract, ALU.mult)
            return ins

        pres = {}

        def pre_step(d, k):
            if k == 0:
                pres["ch"] = Chain(dve, s["own_r"], d * PRE_MARKS)
            ch = pres["ch"]
            if k == 0:
                for b in range(B):
                    x = X[:, bass.ds(NBLK * b + 2 * d, 2), :].rearrange("p n (h w) -> p n h w", w=16)
                    a = CTXH[:, NBLK * b:NBLK * b + 8, bass.ds(2 * d, 2), :].rearrange("p h n w -> p n h w")
                    ch.mark(V.tensor_tensor(X1[:, 2 * b:2 * b + 2, :].rearrange("p n (h w) -> p n h w", w=16),
                                            x, a, ALU.add))
                ch.settle()
                stats(ch, X1)
            if k == AT["norm1"]:
                dve.wait_ge(s["t3"], d)
                normed(d, 0, X1, XN).then_inc(s["xn1"], 1)
            if k == AT["mix_prev"]:
                dve.wait_ge(s["xnt"], d + 1)
                dve.wait_ge(s["r_psum"], d)
                prev = XNT[:, :, 0:256]
                for n, x in enumerate((XR, XK)):
                    ch.mark(V.tensor_scalar(x[:], prev, MU1[:, n:n + 1], None, ALU.mult))
            if k == AT["mix_now"]:
                now = XNT[:, :, 1:257]
                ch.settle()
                for n, x in enumerate((XR, XK)):
                    ch.mark(V.scalar_tensor_tensor(x[:], now, t["mu"][:, n:n + 1], x[:], ALU.mult, ALU.add))
                V.tensor_copy(XNT[:, :, 0:1], XNT[:, :, 256:257]).then_inc(s["mixed"], 1)
            if k == AT["square"]:
                dve.wait_ge(s["relu"], d + 1)
                V.tensor_tensor(KA[:], KR[:], KR[:], ALU.mult).then_inc(s["ka"], 1)
            if k == AT["channel_out"]:
                dve.wait_ge(s["v_psum"], d + 1)
                dve.wait_ge(s["sig"], d + 1)
                ch.mark(V.tensor_tensor(U[:], RS[:], R0[:].rearrange("p (g d) -> p g d", g=4), ALU.mult))
                ch.settle()
                dve.wait_ge(s["acc_done"], d)
                ch.mark(V.tensor_tensor(X2[:], X1[:], U[:], ALU.add))
            if k == AT["stats2"]:
                ch.settle()
                stats(ch, X2)
            if k == AT["norm2"]:
                ch.mark(normed(d, 1, X2, A))
                ch.settle()
                stats(ch, A)
            if k == AT["norm3"]:
                ch.mark(normed(d, 2, A, HH))
                ch.settle()
                ch.mark(V.tensor_tensor(HH[:], HH[:], wide(LNW), ALU.mult))
            h0, h1 = HH[:, 0:2, :], HH[:, 2:4, :]
            if k == AT["spiral1"]:
                ch.settle()
                ch.mark(V.tensor_tensor(HH[:], HH[:], wide(LNB), ALU.add))
                ch.settle()
                ch.mark(V.tensor_tensor(U[:, 0:2, :], h0, wide2(CI[:]), ALU.add))
                ch.mark(V.tensor_tensor(U[:, 2:4, :], h0, wide2(CR[:]), ALU.mult))
            if k == AT["spiral2"]:
                ch.settle()
                ch.mark(V.tensor_tensor(U[:, 2:4, :], U[:, 2:4, :], wide2(CI2[:]), ALU.add))
                ch.settle()
                ch.mark(V.tensor_tensor(U[:, 2:4, :], U[:, 2:4, :], h1, ALU.add))
                ch.settle()
                ch.mark(V.tensor_tensor(Y[:], U[:], HH[:], ALU.mult))
            if k == AT["stats4"]:
                ch.settle()
                V.tensor_tensor(Y[:], Y[:], A[:], ALU.add).then_inc(s["y_done"], 1)
                dve.wait_ge(s["y_done"], d + 1)
                stats(ch, Y)
            if k == AT["norm4"]:
                ch.mark(normed(d, 3, Y, XN))
                ch.settle()
                ch.mark(V.tensor_tensor(XN[:], XN[:], wide(LNW), ALU.mult))
                ch.settle()
                V.tensor_tensor(XN[:], XN[:], wide(LNB), ALU.add).then_inc(s["h2"], 1)
            if k == AT["x3"]:
                dve.wait_ge(s["l2_psum"], d + 1)
                dve.wait_ge(s["acc_done"], d + 1)
                V.tensor_tensor(X3[:], ACC[:], R0[:].rearrange("p (g d) -> p g d", g=4), ALU.add
                                ).then_inc(s["x3"], 1)
                dve.wait_ge(s["x3"], d + 1)
                stats(ch, X3)
            if k == AT["norm5"]:
                normed(d, 4, X3, XN).then_inc(s["xm"], 1)
            if k == 23:
                pres["n"] = ch.k

        def gates(c):
            dve.wait_ge(s["xmt"], c + 1)
            V.tensor_copy(XMH[:], XMT[:]).then_inc(s["xm_parts"], 1)
            dve.wait_ge(s["xm_parts"], c * 2 + 1)
            V.tensor_tensor(XML[:], XMT[:], XMH[:].bitcast(F32), ALU.subtract).then_inc(s["xm_parts"], 1)
            ch = Chain(dve, s["own_g"], c * ROUTE_MARKS)
            dve.wait_ge(s["logits"], c + 1)
            ch.mark(V.tensor_copy(LG[:], R0[:, 0:32].rearrange("p (g e) -> p g e", g=4)))
            ch.settle()
            V.memset(HOLD[:, 0:1], 0.0)
            for g in range(4):
                ch.mark(V.max(M8[:, g, :], LG[:, g, :]))
            ch.settle()
            V.memset(HOLD[:, 1:2], 0.0)
            for g in range(4):
                ch.mark(V.max_index(I8[:, g, :], M8[:, g, :], LG[:, g, :]))
            V.tensor_tensor(DL[:], M8[:, :, 1], M8[:, :, 0], ALU.subtract).then_inc(s["gap"], 1)
            ch.settle()
            ch.mark(V.tensor_copy(IF[:], I8[:, :, 0:2]))
            ch.settle()
            iota = t["iota"][:].rearrange("p (o e) -> p o e", o=1).to_broadcast([128, 4, NE])
            for n, eq in enumerate((E1, E2)):
                ch.mark(V.tensor_tensor(eq[:], iota, IF[:, :, n:n + 1].to_broadcast([128, 4, NE]), ALU.is_equal))
            dve.wait_ge(s["gap_exp"], c + 1)
            ch.mark(V.tensor_scalar(SM[:], EX[:], 1.0, None, ALU.add))
            ch.settle()
            ch.mark(V.reciprocal(RW[:], SM[:]))
            ch.settle()
            ch.mark(V.tensor_tensor(EW[:], EX[:], RW[:], ALU.mult))
            ch.settle()
            for eq, w in ((E1, RW), (E2, EW)):
                ch.mark(V.tensor_tensor(eq[:], eq[:], w[:].rearrange("p (g o) -> p g o", o=1)
                                        .to_broadcast([128, 4, NE]), ALU.mult))
            ch.settle()
            ch.mark(V.tensor_tensor(G[:], E1[:], E2[:], ALU.add))
            ch.settle()
            assert ch.k == ROUTE_MARKS, ch.k

        def add_expert(c, e):
            dve.wait_ge(s["down"], c * NE + (e + 1))
            if e:
                dve.wait_ge(s["added"], c * NE + (e + 2))
            else:
                dve.wait_ge(s["stored"], c * 32 + 16)
            for g in range(4):
                ins = V.scalar_tensor_tensor(OUT[:, g, :], PY[e % 2][:, 128 * g:128 * g + 128], G[:, g, e:e + 1],
                                             (OUT if e else X3)[:, g, :], ALU.mult, ALU.add)
            ins.then_inc(s["added"], 1)

        def part(c, k, moe, pre):
            e, m = k // 3, k % 3
            if moe:
                n = c * PARTS + (k + 1)
                rows = MROWS[m]
                dve.wait_ge(s["silu"], n + 2)
                dve.wait_ge(s["up_v"], n)
                if m == 0 and e >= 2:
                    dve.wait_ge(s["down"], c * NE + (e - 1))
                V.tensor_tensor(HM[0:rows, e % 2, m, :], SU[0:rows, k % 2, :], PVV[k % 2][0:rows, :], ALU.mult
                                ).then_inc(s["hm"], 1)
                if m == 0 and e >= 2:
                    add_expert(c, e - 2)
            if pre:
                pre_step(c + 1, k)
            if not moe and k == AT["norm1"]:
                spiral_constants()

        def after(c):
            add_expert(c, NE - 2)
            add_expert(c, NE - 1)

        run(dve, gates, part, after)
        assert pres["n"] == PRE_MARKS, pres["n"]


def program(nc, a, out):
    ctx = ExitStack()
    with ctx:
        X = ctx.enter_context(nc.sbuf_tensor("x", [128, B * NBLK, D], F32))
        CTXH = ctx.enter_context(nc.sbuf_tensor("context", [128, PAIRS, NBLK, 16], F32))
        ID = ctx.enter_context(nc.sbuf_tensor("sb_ident", [128, 128], F32))
        loaded = ctx.enter_context(nc.semaphore("loaded"))
        weights, loads = tail_weights(nc, ctx, a)
        with ExitStack() as attn:
            attention_block(nc, attn, [a[n] for n in ("x", "Wq", "bq", "Wk", "bk", "Wv", "bv", "rel", "ident",
                                                      "flip", "sel", "rows")], X, CTXH, ID, loads, loaded)
        with ExitStack() as tail:
            tail_block(nc, tail, weights, len(loads), loaded, ID, X, CTXH, out)


def kernel(**inputs):
    import numpy as _np
    import concourse.bacc as _bacc
    from concourse import mybir as _mybir
    from concourse.bass_utils import run_bass_kernel_spmd as _run

    g = inputs
    arrays = {
        "x": g["L0_attn_hidden_states"], "Wq": g["L0_attn_Wq"], "bq": g["L0_attn_bq"], "Wk": g["L0_attn_Wk"],
        "bk": g["L0_attn_bk"], "Wv": g["L0_attn_Wv"], "bv": g["L0_attn_bv"], "rel": g["L0_attn_rel_bias"],
        "W_r": g["L0_ffn_W_r"].T, "W_k": g["L0_ffn_W_k"].T, "W_v": g["L0_ffn_W_v"].T,
        "mu_r": g["L0_ffn_mu_r"], "mu_k": g["L0_ffn_mu_k"],
        "lmlg": g["L1_attn_lmlg"], "theta": g["L1_attn_theta"], "init": g["L1_attn_last_conv_init"],
        "ln_w": g["L1_attn_ln_w"], "ln_b": g["L1_attn_ln_b"], "l1_w1": g["L1_attn_w1"], "b1": g["L1_attn_b1"].reshape(4, 128).T,
        "l1_w2": g["L1_attn_w2"], "b2": g["L1_attn_b2"],
        "gate_w": g["L1_ffn_gate_w"].T, "w1": g["L1_ffn_w1"].transpose(2, 0, 1),
        "w3": g["L1_ffn_w3"].transpose(2, 0, 1), "w2": g["L1_ffn_w2"].transpose(0, 2, 1),
        "ident": _np.eye(128, dtype=_np.float32), "flip": _np.eye(128, dtype=_np.float32)[::-1],
        "sel": bias_selectors(), "rows": step_rows(), "iota": _np.arange(NE, dtype=_np.float32),
    }
    arrays = {f"in_{n}": _np.ascontiguousarray(a) for n, a in arrays.items()}
    nc = _bacc.Bacc("TRN2", target_bir_lowering=False, num_devices=1)
    aps = {n[3:]: nc.dram_tensor(n, a.shape, _mybir.dt.from_np(a.dtype), kind="ExternalInput").ap()
           for n, a in arrays.items()}
    out = nc.dram_tensor("out", (B, S, D), F32, kind="ExternalOutput").ap()
    program(nc, aps, out)
    r = _run(nc, [arrays], core_ids=[0])
    return r.results[0]["out"]
```
